# Optimizing a Trainium2 kernel written in Bass

```python
import numpy as np
import jax
import jax.numpy as jnp

def _softmax(x, axis=-1):
    return jax.nn.softmax(x, axis=axis)

def _gelu(x):
    return jax.nn.gelu(x, approximate=True)

def _silu(x):
    return jax.nn.silu(x)

def _sigmoid(x):
    return jax.nn.sigmoid(x)

def _layernorm(x, axis=-1, eps=1e-05):
    m = jnp.mean(x, axis=axis, keepdims=True)
    v = jnp.var(x, axis=axis, keepdims=True)
    return (x - m) / jnp.sqrt(v + eps)

def _scatter_add(tgt, idx, src, axis=0):
    return tgt.at[idx].add(src)

def _segment_sum(src, seg, n):
    return jax.ops.segment_sum(src, seg, n)
kernel_name = 'mk_seq_postln_d1_jaxref_r8_22d9c9'

def setup_inputs(seed: int=0):
    np.random.seed(seed)
    _w = jnp.asarray

    def _L0_attn_setup():
        import jax, jax.numpy as jnp
        import numpy as np
        B, S, E, H, Dh = (2, 256, 128, 16, 64)
        key = jax.random.key(seed)
        ks = jax.random.split(key, 8)
        w = 0.02
        return {'x': jax.random.normal(ks[0], (B, S, E), jnp.float32), 'Wq': jax.random.normal(ks[1], (H, Dh, E), jnp.float32) * w, 'bq': jax.random.normal(ks[2], (H, Dh), jnp.float32) * w, 'Wk': jax.random.normal(ks[3], (H, Dh, E), jnp.float32) * w, 'bk': jax.random.normal(ks[4], (H, Dh), jnp.float32) * w, 'Wv': jax.random.normal(ks[5], (H, Dh, E), jnp.float32) * w, 'bv': jax.random.normal(ks[6], (H, Dh), jnp.float32) * w, 'proj': jax.random.normal(ks[7], (H * Dh, E), jnp.float32) * w}
    _L0_attn_in = _L0_attn_setup()

    def _L0_ffn_setup():
        import jax, jax.numpy as jnp
        import numpy as np
        B, S, H = (2, 128, 128)
        E, I = (16, 64)
        TOP_K = 2
        N_SHARED = 2
        SCALE = 1.0
        IS = I * N_SHARED
        key = jax.random.key(seed)
        ks = jax.random.split(key, 8)
        sd = 0.02
        return {'hidden_states': jax.random.normal(ks[0], (B, S, H), jnp.float32), 'gate_w': jax.random.normal(ks[1], (E, H), jnp.float32) * sd, 'w_gate': jax.random.normal(ks[2], (E, H, I), jnp.float32) * sd, 'w_up': jax.random.normal(ks[3], (E, H, I), jnp.float32) * sd, 'w_down': jax.random.normal(ks[4], (E, I, H), jnp.float32) * sd, 'ws_gate': jax.random.normal(ks[5], (H, IS), jnp.float32) * sd, 'ws_up': jax.random.normal(ks[6], (H, IS), jnp.float32) * sd, 'ws_down': jax.random.normal(ks[7], (IS, H), jnp.float32) * sd}
    _L0_ffn_in = _L0_ffn_setup()
    _d = {'L0_attn_x': _L0_attn_in['x'], 'L0_attn_Wq': _L0_attn_in['Wq'], 'L0_attn_bq': _L0_attn_in['bq'], 'L0_attn_Wk': _L0_attn_in['Wk'], 'L0_attn_bk': _L0_attn_in['bk'], 'L0_attn_Wv': _L0_attn_in['Wv'], 'L0_attn_bv': _L0_attn_in['bv'], 'L0_attn_proj': _L0_attn_in['proj'], 'L0_ffn_gate_w': _L0_ffn_in['gate_w'], 'L0_ffn_w_gate': _L0_ffn_in['w_gate'], 'L0_ffn_w_up': _L0_ffn_in['w_up'], 'L0_ffn_w_down': _L0_ffn_in['w_down'], 'L0_ffn_ws_gate': _L0_ffn_in['ws_gate'], 'L0_ffn_ws_up': _L0_ffn_in['ws_up'], 'L0_ffn_ws_down': _L0_ffn_in['ws_down']}
    _x0 = _d['L0_attn_x']
    _d['L0_attn_x'] = jax.random.normal(jax.random.fold_in(jax.random.key(seed), 1), (4, 1024, 128), dtype=_x0.dtype)
    del _x0
    return _d

def reference(L0_attn_x, L0_attn_Wq, L0_attn_bq, L0_attn_Wk, L0_attn_bk, L0_attn_Wv, L0_attn_bv, L0_attn_proj, L0_ffn_gate_w, L0_ffn_w_gate, L0_ffn_w_up, L0_ffn_w_down, L0_ffn_ws_gate, L0_ffn_ws_up, L0_ffn_ws_down):

    def _L0_attn_ref(x, Wq, bq, Wk, bk, Wv, bv, proj):
        import jax, jax.numpy as jnp
        import numpy as np
        B, S, E, H, Dh = (2, 256, 128, 16, 64)
        b, s, e = x.shape
        h, dh, _ = Wq.shape
        scale = jnp.sqrt(jnp.asarray(dh, x.dtype))
        q = jnp.einsum('bse,hde->bhsd', x, Wq) + bq[None, :, None, :]
        k = jnp.einsum('bse,hde->bhsd', x, Wk) + bk[None, :, None, :]
        v = jnp.einsum('bse,hde->bhsd', x, Wv) + bv[None, :, None, :]
        causal = jnp.triu(jnp.ones((s, s), bool), 1)
        scores = jnp.einsum('bhsd,bhtd->bhst', q, k) / scale
        scores = jnp.where(causal[None, None], -jnp.inf, scores)
        att = jax.nn.softmax(scores, axis=-1) / scale
        z = jnp.einsum('bhst,bhtd->bhsd', att, v)
        z = z.reshape(b, s, h * dh)
        return z @ proj

    def _L0_ffn_ref(hidden_states, gate_w, w_gate, w_up, w_down, ws_gate, ws_up, ws_down):
        import jax, jax.numpy as jnp
        import numpy as np
        B, S, H = (2, 128, 128)
        E, I = (16, 64)
        TOP_K = 2
        N_SHARED = 2
        SCALE = 1.0
        IS = I * N_SHARED
        b, s, h = hidden_states.shape
        x = hidden_states.reshape(-1, h)
        T = x.shape[0]
        logits = jnp.einsum('th,eh->te', x.astype(jnp.float32), gate_w.astype(jnp.float32))
        scores = jax.nn.softmax(logits, axis=-1)
        topk_w, topk_idx = jax.lax.top_k(scores, TOP_K)
        topk_w = topk_w * SCALE
        combine = jnp.zeros((T, E), jnp.float32).at[jnp.arange(T)[:, None], topk_idx].add(topk_w)
        g = jnp.einsum('th,ehi->tei', x, w_gate)
        u = jnp.einsum('th,ehi->tei', x, w_up)
        act = jax.nn.silu(g) * u
        routed = jnp.einsum('tei,eih,te->th', act, w_down, combine)
        sg = jax.nn.silu(x @ ws_gate) * (x @ ws_up)
        shared = sg @ ws_down
        return (routed + shared).reshape(b, s, h)
    x = L0_attn_x
    x = _layernorm(x + _L0_attn_ref(x, L0_attn_Wq, L0_attn_bq, L0_attn_Wk, L0_attn_bk, L0_attn_Wv, L0_attn_bv, L0_attn_proj), axis=-1)
    x = _layernorm(x + _L0_ffn_ref(x, L0_ffn_gate_w, L0_ffn_w_gate, L0_ffn_w_up, L0_ffn_w_down, L0_ffn_ws_gate, L0_ffn_ws_up, L0_ffn_ws_down), axis=-1)
    return x

_drawn_inputs = setup_inputs


def setup_inputs(seed=0):
    import zlib

    import numpy as np

    out = dict(_drawn_inputs(seed))
    spreads = {}
    factors = {'L0_attn_Wq': 8.0,
     'L0_attn_bq': 8.0,
     'L0_attn_Wk': 8.0,
     'L0_attn_bk': 8.0,
     'L0_attn_Wv': 8.0,
     'L0_attn_bv': 8.0,
     'L0_attn_proj': 8.0,
     'L0_ffn_gate_w': 8.0,
     'L0_ffn_w_gate': 8.0,
     'L0_ffn_w_up': 8.0,
     'L0_ffn_w_down': 8.0,
     'L0_ffn_ws_gate': 8.0,
     'L0_ffn_ws_up': 8.0,
     'L0_ffn_ws_down': 8.0}
    for name, (base, spread) in spreads.items():
        noise = np.random.default_rng([zlib.crc32(name.encode()), seed]).standard_normal(out[name].shape)
        drawn = base * np.exp(spread * noise) if base else spread * noise
        out[name] = jnp.asarray(drawn.astype(out[name].dtype))
    for name, factor in factors.items():
        out[name] = (out[name] * factor).astype(out[name].dtype)
    return out
```

```python
from contextlib import ExitStack

import concourse.bass as bass
from concourse import mybir

F32 = mybir.dt.float32
F32R = mybir.dt.float32r
BF16 = mybir.dt.bfloat16
U32 = mybir.dt.uint32
ALU = mybir.AluOpType
ACT = mybir.ActivationFunctionType
AX = mybir.AxisListType

P = 128
B, S, E = 4, 1024, 128
H, DH = 16, 64
HP = H // 2
NPAIR = B * HP
QT = S // P
STEPS = 2 * QT
T_ALL = B * S
SCALE = 1.0 / DH ** 0.5
MASKED = -3.0e38
WCOLS = 6 * P
WROW = WCOLS + 4
NE, NI = 16, 64
NT = NE * NI // P + 1
CHUNK = 512
NCH = T_ALL // CHUNK
TT = CHUNK // P
EPS = 1e-5


def at_least(engine, semaphore, value):
    if isinstance(value, int) and value <= 0:
        return
    engine.wait_ge(semaphore, value)


def at_least_apart(engine, semaphore, value, passed):
    if isinstance(value, int) and value <= 0:
        return
    engine.wait_ge(semaphore, value).then_inc(passed, 1)


def before(n, s, back):
    s2 = s - back
    return (n, 0, s2) if s2 >= 0 else (n - 1, 1, s2 + STEPS)


def exists(n):
    return not isinstance(n, int) or 0 <= n < NPAIR


T_LAG = 3
V_LAG = 7
RING = 4
Z_STEPS = ((6 + V_LAG) % STEPS, (14 + V_LAG) % STEPS)
OUT_STEP = 11

T_USES = [(s, b) for s in range(STEPS) for b in range(s // 2 // 4 + 1)]
NUSE = len(T_USES)
USE_AT = {use: i for i, use in enumerate(T_USES)}
BY_ACT = [(s + b) % 2 == 1 for s, b in T_USES]
HALF = NUSE // 2
SEEN = [sum(a == BY_ACT[i] for a in BY_ACT[:i + 1]) for i in range(NUSE)]


def split_inputs(nc, xs, xraw, wbuf, w_loaded, x_in, wsp_d, xT, wq, wk, wv, bq, bk, bv, early):
    with ExitStack() as c:
        wraw = c.enter_context(nc.sbuf_tensor("wraw", [P, 3, HP, P], F32))
        braw = c.enter_context(nc.sbuf_tensor("braw", [P, 3, HP], F32))
        wsp = c.enter_context(nc.sbuf_tensor("wsp", [P, HP, WROW], F32R))
        w_in = c.enter_context(nc.semaphore("w_in"))
        b_in = c.enter_context(nc.semaphore("b_in"))
        hi_done = c.enter_context(nc.semaphore("split_hi_done"))
        lo_done = c.enter_context(nc.semaphore("split_lo_done"))
        w_out = c.enter_context(nc.semaphore("w_out"))
        whi = [wsp[:, :, (2 * t) * P:(2 * t + 1) * P] for t in range(3)]
        wlo = [wsp[:, :, (2 * t + 1) * P:(2 * t + 2) * P] for t in range(3)]
        with nc.Block() as block:
            @block.sync
            def _(sp):
                for t, w in enumerate((wq, wk, wv)):
                    sp.dma_start(wraw[:, t], w).then_inc(w_in, 16)
                for t, b in enumerate((bq, bk, bv)):
                    sp.dma_start(braw[:, t], b).then_inc(b_in, 16)
                sp.wait_ge(hi_done, 1)
                sp.wait_ge(lo_done, 1)
                for k in range(2):
                    sp.dma_start(wbuf[k][:, :].bitcast(F32), wsp[:, k, :].bitcast(F32)).then_inc(w_loaded[k], 16)
                sp.dma_start(wsp_d.rearrange("n p w -> p n w"), wsp[:, :, :].bitcast(F32)).then_inc(w_out, 16)
                for buffer, source in early[1]:
                    sp.dma_start(buffer, source).then_inc(early[0], 16)
                sp.wait_ge(w_out, 16)
                sp.wait_ge(w_loaded[0], 16)
                sp.wait_ge(w_loaded[1], 16)

            @block.scalar
            def _(act):
                act.dma_start(xraw[:, 0:S], xT[:, 0:S]).then_inc(x_in[0], 16)
                act.dma_start(xraw[:, S:T_ALL], xT[:, S:T_ALL]).then_inc(x_in[1], 16)
                act.wait_ge(w_in, 48)
                for t in range(3):
                    last = nc.scalar.activation(whi[t], wraw[:, t], ACT.Copy, scale=SCALE if t == 0 else 1.0)
                last.then_inc(hi_done, 1)
                act.wait_ge(x_in[0], 16)
                nc.scalar.activation(xs[:, 0, 0:S], xraw[:, 0:S], ACT.Copy).then_inc(hi_done, 1)

            @block.vector
            def _(dve):
                dve.wait_ge(b_in, 48)
                biases = wsp[:, :, WCOLS:WROW].bitcast(F32)
                nc.vector.memset(biases[:, :, 3:4], 0.0)
                for t in range(3):
                    nc.vector.tensor_scalar(biases[:, :, t:t + 1], braw[:, t].unsqueeze(2),
                                            SCALE if t == 0 else 1.0, None, ALU.mult)
                dve.wait_ge(hi_done, 1)
                for t in range(3):
                    last = nc.vector.scalar_tensor_tensor(out=wlo[t], in0=wraw[:, t], scalar=SCALE if t == 0 else 1.0,
                                                          in1=whi[t].bitcast(F32), op0=ALU.mult, op1=ALU.subtract)
                last.then_inc(lo_done, 1)
                dve.wait_ge(hi_done, 2)
                nc.vector.tensor_tensor(xs[:, 1, 0:S], xraw[:, 0:S], xs[:, 0, 0:S].bitcast(F32), ALU.subtract)


def attention(nc, xs, xraw, wbuf, w_loaded, x_in, wsp_d, proj, y_all):
    with ExitStack() as c:
        def sb(name, shape, dt):
            return c.enter_context(nc.sbuf_tensor(name, shape, dt))

        def ps(name, shape):
            return c.enter_context(nc.psum_tensor(name, shape, F32))

        def sem(name):
            return c.enter_context(nc.semaphore(name))

        stage = sb("stage", [P, 2, 2, S], F32R)
        qd = [sb(f"qd{i}", [P, 2, 2, S], F32R) for i in range(2)]
        k2 = [sb(f"k2{i}", [P, 2, S], F32R) for i in range(2)]
        vt = sb("vt", [P, S], F32)
        v = [sb(f"v{i}", [P, QT, P], F32) for i in range(2)]
        probs = sb("probs", [P, 4, S], F32)
        pt = sb("pt", [P, 2, 2, S], F32)
        zt = sb("zt", [P, S], F32)
        zs = sb("zs", [P, 2, S // 2], F32)
        pw = sb("pw", [P, HP, E], F32)
        negmax = sb("negmax", [P, RING], F32)
        rowsum = sb("rowsum", [P, RING], F32)
        rinv = sb("rinv", [P, RING], F32)
        ident = sb("ident", [P, P], F32)
        identb = sb("identb", [P, P], BF16)
        maskb = sb("maskb", [P, P], BF16)

        ps_s = ps("ps_s", [P, 2, S])
        ps_t = ps("ps_t", [P, 2, 512])
        ps_m = ps("ps_m", [P, 512])
        ps_z = ps("ps_z", [P, 512])

        consts = sem("consts")
        passed = sem("passed")
        x_split = sem("x_split")
        xhi_done = sem("xhi_done2")
        proj_done = sem("proj_done")
        hi_done = sem("hi_done")
        lo_done = sem("lo_done")
        q_loaded = sem("q_loaded")
        k_loaded = sem("k_loaded")
        scores_done = sem("scores_done")
        max_done = sem("max_done")
        exp_done = sem("exp_done")
        rinv_done = sem("rinv_done")
        probs_done = sem("probs_done")
        t_done = sem("t_done")
        evac_act = sem("evac_act")
        evac_dve = sem("evac_dve")
        pv_done = sem("pv_done")
        z_done = sem("z_done")
        pw_loaded = sem("pw_loaded")
        z_moved = sem("z_moved")
        out_done = sem("out_done2")
        y_done = sem("y_done")

        FIRST = 0

        def bank_of(k, j):
            if isinstance(k, int) and k == FIRST:
                return [ps_s[:, 0, 0:512], ps_s[:, 0, 512:S], ps_s[:, 1, 0:512], ps_s[:, 1, 512:S],
                        ps_t[:, 0, :], ps_t[:, 1, :], ps_z[:, :], ps_m[:, :]][j]
            return ps_m[:, :]

        def evacuated(n, use):
            return (evac_act if BY_ACT[use] else evac_dve), n * HALF + SEEN[use]

        def over_pairs(engine, body, tail):
            body(0, 0)
            body(1, 1)
            with engine.Fori(1, NPAIR // 2 - 1) as k:
                body(k * 2, 0)
                body(k * 2 + 1, 1)
            body(NPAIR - 2, 0)
            body(NPAIR - 1, 1)
            if tail:
                for s in range(V_LAG + 1):
                    tail(s)

        with nc.Block() as block:
            @block.gpsimd
            def _(pool):
                nc.gpsimd.memset(ident[:, :], 0.0)
                nc.gpsimd.memset(maskb[:, :], 0.0).then_inc(consts, 1)
                pool.wait_ge(consts, 1)
                nc.gpsimd.affine_select(out=ident[:, :], in_=ident[:, :], compare_op=ALU.not_equal, fill=1.0,
                                        base=0, pattern=[[-1, P]], channel_multiplier=1)
                nc.gpsimd.affine_select(out=maskb[:, :], in_=maskb[:, :], compare_op=ALU.is_ge, fill=MASKED,
                                        base=0, pattern=[[-1, P]], channel_multiplier=1).then_inc(consts, 1)
                pool.wait_ge(consts, 2)
                nc.gpsimd.tensor_copy(identb[:, :], ident[:, :]).then_inc(consts, 1)

                def body(n, par):
                    for s in range(STEPS):
                        at_least_apart(pool, rinv_done, n * STEPS + s + 1, passed)
                        row = probs[:, s % RING, 0:(s // 2 + 1) * P]
                        nc.gpsimd.tensor_scalar(row, row, rinv[:, s % RING:s % RING + 1], SCALE,
                                                ALU.mult, ALU.mult).then_inc(probs_done, 1)

                over_pairs(pool, body, None)

            @block.sync
            def _(sp):
                def load_weights(k, par):
                    at_least(sp, hi_done, k * 6 - 6)
                    at_least(sp, lo_done, k * 6 - 6)
                    p = k % HP
                    sp.dma_start(wbuf[par][:, :].bitcast(F32),
                                 wsp_d[bass.ds(p, 1), :, :].rearrange("o p w -> p (o w)")
                                 ).then_inc(w_loaded[par], 16)

                def load_q(k, par):
                    at_least(sp, lo_done, k * 6 + 2)
                    at_least(sp, scores_done, k * STEPS - STEPS)
                    for head in range(2):
                        for half in range(2):
                            sp.dma_start(qd[par][half * DH:(half + 1) * DH, head].bitcast(F32),
                                         stage[head * DH:(head + 1) * DH, 0].bitcast(F32)).then_inc(q_loaded, 16)

                def load_k(k, par):
                    at_least(sp, lo_done, k * 6 + 4)
                    for head in range(2):
                        for half in range(2):
                            sp.dma_start(k2[par][half * DH:(half + 1) * DH, head].bitcast(F32),
                                         stage[head * DH:(head + 1) * DH, 1, half].bitcast(F32)
                                         ).then_inc(k_loaded, 16)

                def move_z(n):
                    at_least(sp, z_done, n * 2 + 2)
                    at_least(sp, out_done, n)
                    for head in range(2):
                        for odd in range(2):
                            sp.dma_start(zs[odd * DH:(odd + 1) * DH, head],
                                         zt[head * DH:(head + 1) * DH, odd * 512:(odd + 1) * 512]
                                         ).then_inc(z_moved, 16)

                def body(n, par):
                    if exists(n + 2):
                        load_weights(n + 2, par)
                    if exists(n + 1):
                        load_q(n + 1, 1 - par)
                    if exists(n - 1):
                        move_z(n - 1)
                    if exists(n + 1):
                        load_k(n + 1, 1 - par)

                sp.dma_start(pw[:, :, :], proj).then_inc(pw_loaded, 16)
                load_q(0, 0)
                load_k(0, 0)
                over_pairs(sp, body, None)
                move_z(NPAIR - 1)

            @block.tensor
            def _(pe):
                def project(k, par, j):
                    bank = bank_of(k, j)
                    if isinstance(k, int) and k == FIRST:
                        if j >= 6:
                            at_least(pe, hi_done, j - 1)
                    elif j == 0:
                        at_least(pe, w_loaded[par], (k // 2) * 16 + 16)
                        at_least(pe, lo_done, k * 6)
                    elif j <= 4:
                        at_least(pe, lo_done, k * 6 + j)
                    elif j == 5:
                        at_least(pe, hi_done, k * 6 + 5)
                    elif j == 6:
                        at_least(pe, hi_done, k * 6 + 6)
                        at_least(pe, y_done, k - 1)
                    else:
                        at_least(pe, lo_done, k * 6 + 5)
                    if j < 6:
                        which, chunk = divmod(j, 2)
                        w = [wbuf[par][:, (2 * which + i) * P:(2 * which + i + 1) * P] for i in range(2)]
                        x = [xs[:, i, bass.ds((k // HP) * S + chunk * 512, 512)] for i in range(2)]
                        nc.tensor.matmul(bank, w[0], x[0], start=True, stop=False)
                        nc.tensor.matmul(bank, w[0], x[1], start=False, stop=False)
                        nc.tensor.matmul(bank, w[1], x[0], start=False, stop=True).then_inc(proj_done, 1)
                    else:
                        for i in range(4):
                            t = (j - 6) * 4 + i
                            last = nc.tensor.transpose(bank[:, i * P:(i + 1) * P], vt[:, t * P:(t + 1) * P],
                                                       ident[:, :])
                        last.then_inc(proj_done, 1)

                def scores(n, par, s):
                    qt, head = divmod(s, 2)
                    w = (qt + 1) * P
                    if s == 0:
                        at_least(pe, q_loaded, n * 64 + 64)
                        at_least(pe, k_loaded, n * 64 + 64)
                    at_least(pe, exp_done, n * STEPS + s - 1)
                    for c0 in range(0, w, 512):
                        c1 = min(c0 + 512, w)
                        out = ps_s[:, s % 2, c0:c1]
                        keys = k2[par][:, head, c0:c1]
                        last = c1 == w
                        nc.tensor.matmul(out, qd[par][:, head, 0, qt * P:(qt + 1) * P], keys, start=True, stop=False)
                        nc.tensor.matmul(out, qd[par][:, head, 1, qt * P:(qt + 1) * P], keys, start=False,
                                         stop=not last)
                    nc.tensor.matmul(ps_s[:, s % 2, w - P:w], identb[:, :], maskb[:, :], start=False,
                                     stop=True).then_inc(scores_done, 1)

                def transpose_probs(n, s):
                    at_least(pe, probs_done, n * STEPS + s + 1)
                    qt = s // 2
                    for b in range(qt // 4 + 1):
                        use = USE_AT[s, b]
                        n0, old = (n, use - 2) if use >= 2 else (n - 1, use - 2 + NUSE)
                        at_least(pe, *evacuated(n0, old))
                        for kt in range(4 * b, min(4 * b + 4, qt + 1)):
                            last = nc.tensor.transpose(ps_t[:, use % 2, (kt % 4) * P:(kt % 4 + 1) * P],
                                                       probs[:, s % RING, kt * P:(kt + 1) * P], ident[:, :])
                        last.then_inc(t_done, 1)

                def values(n, par, qt):
                    if qt == 0:
                        at_least(pe, lo_done, n * 6 + 6)
                    if qt % 4 == 0:
                        at_least(pe, z_done, n * 2 + qt // 4)
                    uses = [USE_AT[s, b] for s in (2 * qt, 2 * qt + 1) for b in range(qt // 4 + 1)]
                    for by_act in (False, True):
                        at_least(pe, *evacuated(n, max(u for u in uses if BY_ACT[u] == by_act)))
                    for kt in range(qt + 1):
                        for head in range(2):
                            half = slice(head * DH, (head + 1) * DH)
                            last = nc.tensor.matmul(ps_z[half, (qt % 4) * P:(qt % 4 + 1) * P], v[par][:, kt, half],
                                                    pt[:, head, qt % 2, kt * P:(kt + 1) * P],
                                                    start=kt == 0, stop=kt == qt)
                    last.then_inc(pv_done, 1)

                def project_out(n, k):
                    if exists(k):
                        at_least(pe, hi_done, k * 6 + 6)
                    else:
                        at_least(pe, lo_done, NPAIR * 6)
                        at_least(pe, y_done, n)
                    at_least(pe, z_moved, n * 64 + 64)
                    for q in range(HP):
                        for head in range(2):
                            last = nc.tensor.matmul(ps_m[head * DH:(head + 1) * DH, 0:E],
                                                    zs[:, head, q * DH:(q + 1) * DH], pw[:, q, :],
                                                    start=q == 0, stop=q == HP - 1)
                    last.then_inc(out_done, 1)

                def finish(n, par, s):
                    nv, odd, sv = before(n, s, V_LAG)
                    if s % 2 == 1 and exists(nv):
                        values(nv, par ^ odd, sv // 2)
                    if s % 2 == 0 and exists(n) and exists(n + 1):
                        project(n + 1, 1 - par, s // 2)
                    if s == OUT_STEP and exists(n) and exists(n - 1):
                        project_out(n - 1, n + 1)
                    nt, odd, st = before(n, s, T_LAG)
                    if exists(nt):
                        transpose_probs(nt, st)

                def body(n, par):
                    for s in range(STEPS):
                        scores(n, par, s)
                        finish(n, par, s)

                pe.wait_ge(consts, 3)
                pe.wait_ge(pw_loaded, 16)
                for j in range(8):
                    project(FIRST, 0, j)
                pe.wait_ge(lo_done, 6)
                pe.wait_ge(x_split, 1)
                over_pairs(pe, body, lambda s: finish(NPAIR, 0, s))
                project_out(NPAIR - 1, NPAIR + 1)

            def evacuate_probs(engine, by_act, n, s):
                qt, head = divmod(s, 2)
                for b in range(qt // 4 + 1):
                    use = USE_AT[s, b]
                    if BY_ACT[use] != by_act:
                        continue
                    at_least(engine, t_done, n * NUSE + use + 1)
                    at_least(engine, pv_done, n * QT + qt - 1)
                    w = (min(4 * b + 4, qt + 1) - 4 * b) * P
                    dst, src = pt[:, head, qt % 2, b * 512:b * 512 + w], ps_t[:, use % 2, 0:w]
                    if by_act:
                        nc.scalar.copy(dst, src).then_inc(evac_act, 1)
                    else:
                        nc.vector.tensor_copy(dst, src).then_inc(evac_dve, 1)

            def bias_of(par, which):
                return wbuf[par][:, WCOLS + which:WCOLS + which + 1].bitcast(F32)

            @block.scalar
            def _(act):
                def take_hi(k, par, j):
                    if j >= 6:
                        return
                    which, chunk = divmod(j, 2)
                    cols = slice(chunk * 512, (chunk + 1) * 512)
                    at_least(act, proj_done, k * 8 + j + 1)
                    if which < 2:
                        at_least(act, (q_loaded, k_loaded)[which], k * 64)
                        dst = stage[:, which, 0, cols]
                    else:
                        dst = vt[:, cols]
                    nc.scalar.activation(dst, bank_of(k, j), ACT.Identity, bias=bias_of(par, which)).then_inc(hi_done, 1)

                def exponentials(n, s):
                    n4, _, s4 = before(n, s, RING)
                    at_least(act, max_done, n * STEPS + s + 1)
                    if exists(n4):
                        at_least(act, t_done, n4 * NUSE + USE_AT[s4, s4 // 2 // 4] + 1)
                    w = (s // 2 + 1) * P
                    nc.scalar.activation(probs[:, s % RING, 0:w], ps_s[:, s % 2, 0:w], ACT.Exp,
                                         bias=negmax[:, s % RING:s % RING + 1],
                                         accum_out=rowsum[:, s % RING:s % RING + 1]).then_inc(exp_done, 1)

                def evacuate_z(n, half):
                    at_least(act, pv_done, n * QT + 4 * half + 4)
                    if half == 0:
                        at_least(act, z_moved, n * 64)
                    dst = zt[:, :].rearrange("p (o q i) -> p o q i", o=2, q=HP)[:, :, :, half * 32:(half + 1) * 32]
                    src = ps_z[:, :].rearrange("p (i q o) -> p o q i", q=HP, o=2)
                    nc.scalar.copy(dst, src).then_inc(z_done, 1)

                def take_out(n):
                    at_least(act, out_done, n + 1)
                    nc.scalar.copy(y_all[:, bass.ds(n, 1), :].rearrange("p o e -> p (o e)"),
                                   ps_m[:, 0:E]).then_inc(y_done, 1)

                def finish(n, par, s):
                    if s == Z_STEPS[0] and exists(n):
                        evacuate_z(n, 0)
                    if s == Z_STEPS[1] and exists(n - 1):
                        evacuate_z(n - 1, 1)
                    if s % 2 == 0 and exists(n) and exists(n + 1):
                        take_hi(n + 1, 1 - par, s // 2)
                    if s == OUT_STEP and exists(n) and exists(n - 1):
                        take_out(n - 1)
                    nt, _, st = before(n, s, T_LAG)
                    if exists(nt):
                        evacuate_probs(act, True, nt, st)

                def body(n, par):
                    for s in range(STEPS):
                        exponentials(n, s)
                        finish(n, par, s)

                for j in range(8):
                    take_hi(FIRST, 0, j)
                act.wait_ge(x_in[1], 16)
                nc.scalar.activation(xs[:, 0, S:T_ALL], xraw[:, S:T_ALL], ACT.Copy).then_inc(xhi_done, 1)
                over_pairs(act, body, lambda s: finish(NPAIR, 0, s))
                take_out(NPAIR - 1)

            @block.vector
            def _(dve):
                def take_lo(k, par, j):
                    if j in (4, 5):
                        return
                    if j < 4:
                        which, chunk = divmod(j, 2)
                        cols = slice(chunk * 512, (chunk + 1) * 512)
                        at_least(dve, hi_done, k * 6 + j + 1)
                        nc.vector.scalar_tensor_tensor(out=stage[:, which, 1, cols], in0=bank_of(k, j),
                                                       scalar=bias_of(par, which),
                                                       in1=stage[:, which, 0, cols].bitcast(F32),
                                                       op0=ALU.add, op1=ALU.subtract).then_inc(lo_done, 1)
                    else:
                        at_least(dve, proj_done, k * 8 + j + 1)
                        at_least(dve, pv_done, k * QT - QT)
                        tiles = v[par][:, (j - 6) * 4:(j - 6) * 4 + 4, :].rearrange("p t d -> p (t d)")
                        nc.vector.tensor_copy(tiles, bank_of(k, j)).then_inc(lo_done, 1)

                def maxima(n, s):
                    at_least(dve, scores_done, n * STEPS + s + 1)
                    nc.vector.tensor_reduce(negmax[:, s % RING:s % RING + 1], ps_s[:, s % 2, 0:(s // 2 + 1) * P],
                                            AX.X, ALU.max, negate=True).then_inc(max_done, 1)

                def reciprocals(n, s):
                    at_least(dve, exp_done, n * STEPS + s + 1)
                    nc.vector.reciprocal(rinv[:, s % RING:s % RING + 1], rowsum[:, s % RING:s % RING + 1]).then_inc(rinv_done, 1)

                def finish(n, par, s):
                    n1, _, s1 = before(n, s, 1)
                    if exists(n1) and (s == 0 or exists(n)):
                        reciprocals(n1, s1)
                    if s % 2 == 1 and exists(n) and exists(n + 1):
                        take_lo(n + 1, 1 - par, s // 2)
                    nt, _, st = before(n, s, T_LAG)
                    if exists(nt):
                        evacuate_probs(dve, False, nt, st)

                def body(n, par):
                    for s in range(STEPS):
                        maxima(n, s)
                        finish(n, par, s)

                for j in range(8):
                    take_lo(FIRST, 0, j)
                dve.wait_ge(xhi_done, 1)
                nc.vector.tensor_tensor(xs[:, 1, S:T_ALL], xraw[:, S:T_ALL], xs[:, 0, S:T_ALL].bitcast(F32),
                                        ALU.subtract).then_inc(x_split, 1)
                over_pairs(dve, body, lambda s: finish(NPAIR, 0, s))


def mixture(nc, y_all, xc, wraw, wd, gw, early_in, x_tok, out):
    with ExitStack() as c:
        def sb(name, shape, dt=F32):
            return c.enter_context(nc.sbuf_tensor(name, shape, dt))

        def ps(name):
            return c.enter_context(nc.psum_tensor(name, [P, 512], F32))

        def sem(name):
            return c.enter_context(nc.semaphore(name))

        x1 = [sb(f"x1{i}", [P, TT, E]) for i in range(2)]
        xn = [sb(f"xn{i}", [P, 2, CHUNK], F32R) for i in range(2)]
        res = sb("res", [P, TT, E])
        res2 = sb("res2", [P, TT, E])
        ob = [sb(f"ob{i}", [P, TT, E]) for i in range(2)]
        stats = sb("stats", [P, 2, TT, 6])
        mv = sb("mv", [P, 2, TT, 2])
        veps = sb("veps", [P, 2, TT, 1])
        rstd = sb("rstd", [P, 2, TT, 1])
        nmax = sb("nmax", [P, TT, 1])
        lg = sb("lg", [P, TT, NE])
        ex = sb("ex", [P, TT, NE])
        esum = sb("esum", [P, TT, 1])
        einv = sb("einv", [P, TT, 1])
        sc = sb("sc", [P, TT, NE])
        top = sb("top", [P, TT, 8])
        topi = sb("topi", [P, TT, 8], U32)
        topf = sb("topf", [P, TT, 8])
        one = sb("one", [P, TT, 2, NE])
        comb = sb("comb", [P, TT, NE])
        cexp = [sb(f"cexp{i}", [P, TT * NE, NI]) for i in range(2)]
        iota = sb("iota", [P, NE])
        ident = sb("ident3", [P, P])
        epst = sb("epst", [P, TT, 1])
        mhalf = sb("mhalf", [P, TT, 1])
        gs = sb("gs", [P, 2, NE], F32R)
        wgu = sb("wgu", [P, 2, 2, NT, P], F32R)
        sg = sb("sg", [P, 2, CHUNK])
        su = sb("su", [P, 2, CHUNK])
        hid = sb("hid", [P, NT, CHUNK])

        ps_x, ps_d = ps("ps_x"), ps("ps_d")
        ps_b = [ps("ps_b0"), ps("ps_b1")]
        ps_g = [ps("ps_g0"), ps("ps_g1")]
        ps_u = [ps("ps_u0"), ps("ps_u1")]

        consts = sem("consts3")
        passed_dve = sem("passed_dve")
        w_hi = sem("w_hi3")
        w_lo = sem("w_lo3")
        chunk_in = [sem(f"chunk_in{i}") for i in range(2)]
        chain = sem("chain")
        var_done = sem("var_done")
        veps_done = sem("veps_done")
        rstd_done = sem("rstd_done")
        x1_done = sem("x1_done")
        xt_done = sem("xt_done")
        xhi_done = sem("xhi_done")
        xlo_done = sem("xlo_done")
        logit_done = sem("logit_done")
        lg_done = sem("lg_done")
        ex_done = sem("ex_done")
        comb_done = sem("comb_done")
        cexp_done = sem("cexp_done")
        g_done = sem("g_done")
        u_done = sem("u_done")
        b_done = sem("b_done")
        silu_done = sem("silu_done")
        su_done = sem("su_done")
        hid_done = sem("hid_done")
        down_done = sem("down_done")
        out_done = sem("out_done")
        stored = sem("stored")

        def over_chunks(engine, front, experts):
            front(0, 0)
            experts(0, 0, True)
            experts(1, 1, True)
            with engine.Fori(1, NCH // 2 - 1) as k:
                experts(k * 2, 0, True)
                experts(k * 2 + 1, 1, True)
            experts(NCH - 2, 0, True)
            experts(NCH - 1, 1, False)

        with nc.Block() as block:
            @block.sync
            def _(sp):
                def load(c, par):
                    at_least(sp, x1_done, c - 1)
                    sp.dma_start(xc[par][:, :, :], x_tok.rearrange("(c t p) e -> c p t e", t=TT, p=P)
                                 [bass.ds(c, 1)].rearrange("o p t e -> p (o t) e")).then_inc(chunk_in[par], 16)

                def store(c, par):
                    at_least(sp, out_done, c + 1)
                    sp.dma_start(out.rearrange("(c t p) e -> c p t e", t=TT, p=P)
                                 [bass.ds(c, 1)].rearrange("o p t e -> p (o t) e"), ob[par][:, :, :]
                                 ).then_inc(stored, 16)

                load(2, 0)
                store(0, 0)
                load(3, 1)
                store(1, 1)
                with sp.Fori(1, NCH // 2 - 1) as k:
                    load(k * 2 + 2, 0)
                    store(k * 2, 0)
                    load(k * 2 + 3, 1)
                    store(k * 2 + 1, 1)
                store(NCH - 2, 0)
                store(NCH - 1, 1)
                sp.wait_ge(stored, 16 * NCH)

            @block.gpsimd
            def _(pool):
                nc.gpsimd.memset(epst[:, :, :], EPS)
                nc.gpsimd.memset(mhalf[:, :, :], -0.5)
                nc.gpsimd.iota(iota[:, :], pattern=[[1, NE]], base=0, channel_multiplier=0,
                               allow_small_or_imprecise_dtypes=True)
                nc.gpsimd.memset(ident[:, :], 0.0).then_inc(consts, 1)
                pool.wait_ge(consts, 1)
                nc.gpsimd.affine_select(out=ident[:, :], in_=ident[:, :], compare_op=ALU.not_equal, fill=1.0,
                                        base=0, pattern=[[-1, P]], channel_multiplier=1).then_inc(consts, 1)

                def deviation(count, which):
                    at_least(pool, var_done, count)
                    nc.gpsimd.tensor_tensor(veps[:, which], mv[:, which, :, 1:2], epst[:, :, :],
                                            ALU.add).then_inc(veps_done, 1)
                    at_least(pool, veps_done, count)
                    nc.gpsimd.tensor_tensor(rstd[:, which], veps[:, which], mhalf[:, :, :],
                                            ALU.pow).then_inc(rstd_done, 1)

                pool.wait_ge(consts, 2)
                deviation(1, 0)
                deviation(2, 0)
                with pool.Fori(1, NCH - 1) as c:
                    deviation(c * 2 + 1, 1)
                    deviation(c * 2 + 2, 0)
                deviation(2 * NCH - 1, 1)
                deviation(2 * NCH, 1)

            @block.tensor
            def _(pe):
                def front_transpose(c, par):
                    at_least(pe, x1_done, c + 1)
                    at_least(pe, lg_done, c)
                    for t in range(TT):
                        last = nc.tensor.transpose(ps_x[:, t * P:(t + 1) * P], x1[par][:, t, :], ident[:, :])
                    last.then_inc(xt_done, 1)

                def front_logits(c, par):
                    at_least(pe, xhi_done, c + 1)
                    at_least(pe, xlo_done, c + 1)
                    for t in range(TT):
                        for i in range(4):
                            last = nc.tensor.matmul(ps_x[:, t * NE:(t + 1) * NE],
                                                    xn[par][:, i // 2, t * P:(t + 1) * P], gs[:, i % 2, :],
                                                    start=i == 0, stop=i == 3)
                    last.then_inc(logit_done, 1)

                def tile(c, par, j):
                    r = (j + par) % 2
                    for which, banks, done in ((0, ps_g, g_done), (1, ps_u, u_done)):
                        if which == 0:
                            at_least(pe, silu_done, c * NT + max(j - 1, 0))
                        else:
                            at_least(pe, hid_done, c * NT + max(j - 1, 0))
                        for i, (a, b) in enumerate(((0, 0), (0, 1), (1, 0))):
                            last = nc.tensor.matmul(banks[r][:, :], wgu[:, a, which, j, :], xn[par][:, b, :],
                                                    start=i == 0, stop=i == 2)
                        last.then_inc(done, 1)
                    if j < NT - 1:
                        at_least(pe, hid_done, c * NT + max(j - 1, 0))
                        if j == 0:
                            at_least(pe, cexp_done, c + 1)
                        for t in range(TT):
                            last = nc.tensor.transpose(
                                ps_b[r][:, t * P:(t + 1) * P],
                                cexp[par][:, t * NE + 2 * j:t * NE + 2 * j + 2, :].rearrange("p e i -> p (e i)"), ident[:, :])
                        last.then_inc(b_done, 1)

                def down(c, par):
                    at_least(pe, hid_done, c * NT + NT)
                    at_least(pe, out_done, c)
                    for t in range(TT):
                        for j in range(NT):
                            last = nc.tensor.matmul(ps_d[:, t * P:(t + 1) * P], hid[:, j, t * P:(t + 1) * P],
                                                    wd[:, j, :], start=j == 0, stop=j == NT - 1)
                    last.then_inc(down_done, 1)

                def experts(c, par, more):
                    for j in range(NT):
                        tile(c, par, j)
                        if more and j == 3:
                            front_transpose(c + 1, 1 - par)
                        if more and j == 6:
                            front_logits(c + 1, 1 - par)
                    down(c, par)

                def front(c, par):
                    front_transpose(c, par)
                    front_logits(c, par)

                pe.wait_ge(consts, 2)
                pe.wait_ge(w_hi, 1)
                pe.wait_ge(w_lo, 1)
                over_chunks(pe, front, experts)

            @block.scalar
            def _(act):
                def take_xhi(c, par):
                    at_least(act, xt_done, c + 1)
                    nc.scalar.copy(xn[par][:, 0, :], ps_x[:, :]).then_inc(xhi_done, 1)

                def gate_exp(c):
                    at_least(act, lg_done, c + 1)
                    nc.scalar.activation(ex[:, :, :], lg[:, :, :], ACT.Exp).then_inc(ex_done, 1)

                def tile(c, par, j):
                    at_least(act, g_done, c * NT + j + 1)
                    at_least(act, hid_done, c * NT + max(j - 1, 0))
                    r = (j + par) % 2
                    nc.scalar.activation(sg[:, r, :], ps_g[r][:, :], ACT.Silu).then_inc(silu_done, 1)

                def experts(c, par, more):
                    for j in range(NT):
                        tile(c, par, j)
                        if more and j == 4:
                            take_xhi(c + 1, 1 - par)
                    if more:
                        gate_exp(c + 1)

                def front(c, par):
                    take_xhi(c, par)
                    gate_exp(c)

                act.wait_ge(*early_in)
                nc.scalar.copy(gs[:, 0, :], gw[:, :])
                nc.scalar.copy(wgu[:, 0], wraw[:, :, :, :]).then_inc(w_hi, 1)
                over_chunks(act, front, experts)

            @block.vector
            def _(dve):
                def norm_stats(base, which, one_term, other, dst):
                    nc.vector.tensor_tensor(dst[:, :, :].rearrange("p t e -> p (t e)"), one_term,
                                            other[:, :, :].rearrange("p t e -> p (t e)"), ALU.add).then_inc(chain, 1)
                    at_least(dve, chain, base + 1)
                    for t in range(TT):
                        last = nc.vector.bn_stats(stats[:, which, t, :], dst[:, t, :])
                    last.then_inc(chain, 1)
                    at_least_apart(dve, chain, base + 2, passed_dve)
                    for t in range(TT):
                        last = nc.vector.bn_aggr(mv[:, which, t, :], stats[:, which, t, :])
                    last.then_inc(var_done, 1)

                def normalise(count, which, src, dst, done):
                    at_least(dve, rstd_done, count)
                    for t in range(TT):
                        last = nc.vector.tensor_scalar(dst[:, t, :], src[:, t, :], mv[:, which, t, 0:1],
                                                       rstd[:, which, t, 0:1], ALU.subtract, ALU.mult)
                    last.then_inc(done, 1)

                def front_stats(c, par, base):
                    at_least(dve, chunk_in[par], (c // 2) * 16)
                    norm_stats(base, 0, y_all[:, bass.ds(c * TT, TT), :].rearrange("p t e -> p (t e)"), xc[par], res)

                def front_norm(c, par):
                    normalise(1 if isinstance(c, int) and c == 0 else c * 2, 0, res, x1[par], x1_done)

                def take_xlo(c, par):
                    at_least(dve, xhi_done, c + 1)
                    nc.vector.tensor_tensor(xn[par][:, 1, :], ps_x[:, :], xn[par][:, 0, :].bitcast(F32),
                                            ALU.subtract).then_inc(xlo_done, 1)

                def gate_logits(c, base):
                    at_least(dve, logit_done, c + 1)
                    logits = ps_x[:, 0:TT * NE].rearrange("p (t e) -> p t e", t=TT)
                    nc.vector.tensor_reduce(nmax[:, :, 0], logits, AX.X, ALU.max).then_inc(chain, 1)
                    at_least(dve, chain, base + 1)
                    nc.vector.tensor_tensor(lg[:, :, :], logits, nmax[:, :, :].to_broadcast([P, TT, NE]),
                                            ALU.subtract).then_inc(lg_done, 1)

                def gates(c, base):
                    at_least(dve, ex_done, c + 1)
                    nc.vector.tensor_reduce(esum[:, :, 0], ex[:, :, :], AX.X, ALU.add).then_inc(chain, 1)
                    at_least(dve, chain, base + 2)
                    nc.vector.reciprocal(einv[:, :, :], esum[:, :, :]).then_inc(chain, 1)
                    at_least(dve, chain, base + 3)
                    nc.vector.tensor_tensor(sc[:, :, :], ex[:, :, :], einv[:, :, :].to_broadcast([P, TT, NE]),
                                            ALU.mult).then_inc(chain, 1)
                    at_least_apart(dve, chain, base + 4, passed_dve)
                    for t in range(TT):
                        last = nc.vector.max(top[:, t, :], sc[:, t, :])
                    last.then_inc(chain, 1)
                    at_least_apart(dve, chain, base + 5, passed_dve)
                    for t in range(TT):
                        last = nc.vector.max_index(topi[:, t, :], top[:, t, :], sc[:, t, :])
                    last.then_inc(chain, 1)
                    at_least(dve, chain, base + 6)
                    nc.vector.tensor_copy(topf[:, :, :], topi[:, :, :]).then_inc(chain, 1)
                    at_least(dve, chain, base + 7)
                    for t in range(TT):
                        for i in range(2):
                            last = nc.vector.tensor_scalar(one[:, t, i, :], iota[:, :], topf[:, t, i:i + 1],
                                                           top[:, t, i:i + 1], ALU.is_equal, ALU.mult)
                    last.then_inc(chain, 1)
                    at_least(dve, chain, base + 8)
                    nc.vector.tensor_tensor(comb[:, :, :], one[:, :, 0, :], one[:, :, 1, :],
                                            ALU.add).then_inc(comb_done, 1)

                def expand(c, par):
                    at_least(dve, comb_done, c + 1)
                    weights = comb[:, :, :].rearrange("p t e -> p (t e)").unsqueeze(2)
                    nc.vector.tensor_copy(cexp[par][:, :, :], weights.to_broadcast([P, TT * NE, NI])
                                          ).then_inc(cexp_done, 1)

                def tile(c, par, j):
                    r = (j + par) % 2
                    at_least(dve, silu_done, c * NT + j + 1)
                    at_least(dve, u_done, c * NT + j + 1)
                    if j == 0:
                        at_least(dve, down_done, c)
                    if j == NT - 1:
                        nc.vector.tensor_tensor(hid[:, j, :], sg[:, r, :], ps_u[r][:, :],
                                                ALU.mult).then_inc(hid_done, 1)
                        return
                    nc.vector.tensor_tensor(su[:, r, :], sg[:, r, :], ps_u[r][:, :], ALU.mult).then_inc(su_done, 1)
                    at_least(dve, su_done, c * (NT - 1) + j + 1)
                    at_least(dve, b_done, c * (NT - 1) + j + 1)
                    nc.vector.tensor_tensor(hid[:, j, :], su[:, r, :], ps_b[r][:, :], ALU.mult).then_inc(hid_done, 1)

                NORM, GATE = 2, 8
                FRONT = NORM + GATE
                CYCLE = FRONT + NORM

                def last_stats(c, par, base):
                    at_least(dve, down_done, c + 1)
                    norm_stats(base, 1, ps_d[:, :], x1[par], res2)

                def last_norm(c, par, count):
                    at_least(dve, stored, c * 16)
                    normalise(count, 1, res2, ob[par], out_done)

                def experts(c, par, more):
                    first = isinstance(c, int) and c == 0
                    base = FRONT if first else c * CYCLE + FRONT - NORM
                    for j in range(NT):
                        tile(c, par, j)
                        if j == 1:
                            if not first:
                                last_stats(c - 1, 1 - par, base)
                                base = base + NORM
                            if more:
                                front_stats(c + 1, 1 - par, base)
                        if j == 2:
                            if not first:
                                last_norm(c - 1, 1 - par, c * 2 + 1)
                            if more:
                                front_norm(c + 1, 1 - par)
                        if more and j == 4:
                            take_xlo(c + 1, 1 - par)
                        if more and j == 7:
                            gate_logits(c + 1, base + NORM)
                    if more:
                        gates(c + 1, base + NORM)
                        expand(c + 1, 1 - par)
                    else:
                        last_stats(c, par, base)
                        last_norm(c, par, 2 * NCH)

                def front(c, par):
                    front_stats(c, par, 0)
                    front_norm(c, par)
                    take_xlo(c, par)
                    gate_logits(c, NORM)
                    gates(c, NORM)
                    expand(c, par)

                dve.wait_ge(w_hi, 1)
                dve.wait_ge(*early_in)
                dve.wait_ge(consts, 2)
                nc.vector.tensor_tensor(gs[:, 1, :], gw[:, :], gs[:, 0, :].bitcast(F32), ALU.subtract)
                for i in range(2):
                    last = nc.vector.tensor_tensor(wgu[:, 1, i], wraw[:, i], wgu[:, 0, i].bitcast(F32), ALU.subtract)
                last.then_inc(w_lo, 1)
                over_chunks(dve, front, experts)


def layer(nc, xT, x_tok, wq, wk, wv, bq, bk, bv, proj, gate_w, w_gate, w_up, w_down, ws_gate, ws_up, ws_down, out):
    wsp_d = nc.dram_tensor("wsp_d", (HP, P, WROW), F32).ap()
    with ExitStack() as ctx:
        def sb(name, shape):
            return ctx.enter_context(nc.sbuf_tensor(name, shape, F32))

        y_all = sb("y_all", [P, NPAIR, E])
        xc = [sb(f"xc{i}", [P, TT, E]) for i in range(2)]
        wraw = sb("wraw3", [P, 2, NT, P])
        wd = sb("wd", [P, NT, E])
        gw = sb("gw", [P, NE])
        early = ctx.enter_context(nc.semaphore("early"))
        chunks = x_tok.rearrange("(c t p) e -> c p t e", t=TT, p=P)
        loads = [(gw[:, :], gate_w), (wd[:, 0:NT - 1, :], w_down), (wd[:, NT - 1, :], ws_down)]
        for i, (w, ws) in enumerate(((w_gate, ws_gate), (w_up, ws_up))):
            loads += [(wraw[:, i, 0:NT - 1, :], w), (wraw[:, i, NT - 1, :], ws), (xc[i][:, :, :], chunks[i])]

        with ExitStack() as inner:
            xs = inner.enter_context(nc.sbuf_tensor("xs", [P, 2, T_ALL], F32R))
            wbuf = [inner.enter_context(nc.sbuf_tensor(f"wbuf{i}", [P, WROW], F32R)) for i in range(2)]
            w_loaded = [inner.enter_context(nc.semaphore(f"w_loaded{i}")) for i in range(2)]
            x_in = [inner.enter_context(nc.semaphore(f"x_in{i}")) for i in range(2)]
            xraw = y_all[:, :, :].rearrange("p n e -> p (n e)")
            split_inputs(nc, xs, xraw, wbuf, w_loaded, x_in, wsp_d, xT, wq, wk, wv, bq, bk, bv, (early, loads))
            attention(nc, xs, xraw, wbuf, w_loaded, x_in, wsp_d, proj, y_all)
        mixture(nc, y_all, xc, wraw, wd, gw, (early, 16 * len(loads)), x_tok, out)


def kernel(**inputs):
    import numpy as _np
    import concourse.bacc as _bacc
    from concourse import mybir as _mybir
    from concourse.bass_utils import run_bass_kernel_spmd as _run

    a = {k: _np.asarray(v) for k, v in inputs.items()}
    x = a["L0_attn_x"].reshape(T_ALL, E)

    def by_pair(w):
        return w.reshape(HP, P, E).transpose(2, 0, 1)

    def by_tile(w):
        return w.transpose(1, 0, 2).reshape(E, NT - 1, P)

    arrays = {
        "xT": x.T,
        "x_tok": x,
        "wq": by_pair(a["L0_attn_Wq"]),
        "wk": by_pair(a["L0_attn_Wk"]),
        "wv": by_pair(a["L0_attn_Wv"]),
        "bq": a["L0_attn_bq"].reshape(HP, P).T,
        "bk": a["L0_attn_bk"].reshape(HP, P).T,
        "bv": a["L0_attn_bv"].reshape(HP, P).T,
        "proj": a["L0_attn_proj"].reshape(HP, P, E).transpose(1, 0, 2),
        "gate_w": a["L0_ffn_gate_w"].T,
        "w_gate": by_tile(a["L0_ffn_w_gate"]),
        "w_up": by_tile(a["L0_ffn_w_up"]),
        "w_down": a["L0_ffn_w_down"].reshape(NT - 1, P, E).transpose(1, 0, 2),
        "ws_gate": a["L0_ffn_ws_gate"],
        "ws_up": a["L0_ffn_ws_up"],
        "ws_down": a["L0_ffn_ws_down"],
    }
    arrays = {k: _np.ascontiguousarray(v) for k, v in arrays.items()}
    nc = _bacc.Bacc("TRN2", target_bir_lowering=False, num_devices=1)
    args = [nc.dram_tensor(k, v.shape, _mybir.dt.from_np(v.dtype), kind="ExternalInput").ap()
            for k, v in arrays.items()]
    out = nc.dram_tensor("out", (T_ALL, E), _mybir.dt.float32, kind="ExternalOutput").ap()
    layer(nc, *args, out)
    r = _run(nc, [arrays], core_ids=[0])
    return r.results[0]["out"].reshape(B, S, E)
```

```python
from contextlib import ExitStack

import concourse.bass as bass
from concourse import mybir

F32 = mybir.dt.float32
F32R = mybir.dt.float32r
BF16 = mybir.dt.bfloat16
U32 = mybir.dt.uint32
ALU = mybir.AluOpType
ACT = mybir.ActivationFunctionType
AX = mybir.AxisListType

P = 128
B, S, E = 4, 1024, 128
H, DH = 16, 64
HP = H // 2
NPAIR = B * HP
QT = S // P
MT = QT // 2
STEPS = 2 * QT
T_ALL = B * S
SCALE = 1.0 / DH ** 0.5
MASKED = -3.0e38
WCOLS = 6 * P
WROW = WCOLS + 4
NE, NI = 16, 64
NT = NE * NI // P + 1
CHUNK = 512
NCH = T_ALL // CHUNK
TT = CHUNK // P
EPS = 1e-5


def at_least(engine, semaphore, value):
    if isinstance(value, int) and value <= 0:
        return
    engine.wait_ge(semaphore, value)


def at_least_apart(engine, semaphore, value, passed):
    if isinstance(value, int) and value <= 0:
        return
    engine.wait_ge(semaphore, value).then_inc(passed, 1)


def before(n, s, back):
    s2 = s - back
    return (n, 0, s2) if s2 >= 0 else (n - 1, 1, s2 + STEPS)


def exists(n):
    return not isinstance(n, int) or 0 <= n < NPAIR


def chunk_exists(c):
    return not isinstance(c, int) or 0 <= c < NCH


T_LAG = 3
V_LAG = 7
RING = 4
Z_STEPS = ((6 + V_LAG + 2) % STEPS, (14 + V_LAG + 2) % STEPS)
OUT_STEP = 11

T_USES = [(s, b) for s in range(STEPS) for b in range(s // 2 // 4 + 1)]
NUSE = len(T_USES)
USE_AT = {use: i for i, use in enumerate(T_USES)}
BY_ACT = [(s + b) % 2 == 1 for s, b in T_USES]
HALF = NUSE // 2
SEEN = [sum(a == BY_ACT[i] for a in BY_ACT[:i + 1]) for i in range(NUSE)]


def split_inputs(nc, xs, xraw, wbuf, w_loaded, x_in, wsp, wsp_d, w_out, xT, wq, wk, wv, bq, bk, bv):
    with ExitStack() as c:
        wraw = c.enter_context(nc.sbuf_tensor("wraw", [P, 3, HP, P], F32))
        braw = c.enter_context(nc.sbuf_tensor("braw", [P, 3, HP], F32))
        w_in = c.enter_context(nc.semaphore("w_in"))
        b_in = c.enter_context(nc.semaphore("b_in"))
        hi_done = c.enter_context(nc.semaphore("split_hi_done"))
        lo_done = c.enter_context(nc.semaphore("split_lo_done"))
        whi = [wsp[:, :, (2 * t) * P:(2 * t + 1) * P] for t in range(3)]
        wlo = [wsp[:, :, (2 * t + 1) * P:(2 * t + 2) * P] for t in range(3)]
        with nc.Block() as block:
            @block.sync
            def _(sp):
                for t, w in enumerate((wq, wk, wv)):
                    sp.dma_start(wraw[:, t], w).then_inc(w_in, 16)
                for t, b in enumerate((bq, bk, bv)):
                    sp.dma_start(braw[:, t], b).then_inc(b_in, 16)
                sp.wait_ge(hi_done, 3)
                sp.wait_ge(lo_done, 3)
                for k in range(2):
                    sp.dma_start(wbuf[k][:, :].bitcast(F32), wsp[:, k, :].bitcast(F32)).then_inc(w_loaded[k], 16)
                sp.dma_start(wsp_d.rearrange("n p w -> p n w"), wsp[:, :, :].bitcast(F32)).then_inc(w_out, 16)

            @block.scalar
            def _(act):
                act.dma_start(xraw[:, 0:S], xT[:, 0:S]).then_inc(x_in[0], 16)
                act.wait_ge(w_in, 48)
                act.dma_start(xraw[:, S:T_ALL], xT[:, S:T_ALL]).then_inc(x_in[1], 16)
                for t in range(3):
                    nc.scalar.activation(whi[t], wraw[:, t], ACT.Copy, scale=SCALE if t == 0 else 1.0).then_inc(hi_done, 1)
                act.wait_ge(x_in[0], 16)
                nc.scalar.activation(xs[:, 0, 0:S], xraw[:, 0:S], ACT.Copy).then_inc(hi_done, 1)

            @block.vector
            def _(dve):
                dve.wait_ge(b_in, 48)
                biases = wsp[:, :, WCOLS:WROW].bitcast(F32)
                nc.vector.memset(biases[:, :, 3:4], 0.0)
                for t in range(3):
                    nc.vector.tensor_scalar(biases[:, :, t:t + 1], braw[:, t].unsqueeze(2),
                                            SCALE if t == 0 else 1.0, None, ALU.mult)
                for t in range(3):
                    dve.wait_ge(hi_done, t + 1)
                    nc.vector.scalar_tensor_tensor(out=wlo[t], in0=wraw[:, t], scalar=SCALE if t == 0 else 1.0,
                                                   in1=whi[t].bitcast(F32), op0=ALU.mult,
                                                   op1=ALU.subtract).then_inc(lo_done, 1)
                dve.wait_ge(hi_done, 4)
                nc.vector.tensor_tensor(xs[:, 1, 0:S], xraw[:, 0:S], xs[:, 0, 0:S].bitcast(F32), ALU.subtract)


def attention(nc, xs, xraw, wbuf, w_loaded, x_in, pt, wsp_d, w_out, proj, y_all, ident, wgu, gate_up, xc, early):
    with ExitStack() as c:
        def sb(name, shape, dt):
            return c.enter_context(nc.sbuf_tensor(name, shape, dt))

        def ps(name, shape):
            return c.enter_context(nc.psum_tensor(name, shape, F32))

        def sem(name):
            return c.enter_context(nc.semaphore(name))

        stage = sb("stage", [P, 2, 2, S], F32R)
        qd = [sb(f"qd{i}", [P, 2, 2, S], F32R) for i in range(2)]
        k2 = [sb(f"k2{i}", [P, 2, S], F32R) for i in range(2)]
        vt = sb("vt", [P, S], F32)
        v = [sb(f"v{i}", [P, QT, P], F32) for i in range(2)]
        probs = sb("probs", [P, 4, S], F32)
        zt = sb("zt", [P, S], F32)
        zs = sb("zs", [P, 2, S // 2], F32)
        pw = sb("pw", [P, HP, E], F32)
        negmax = sb("negmax", [P, RING], F32)
        rowsum = sb("rowsum", [P, RING], F32)
        rinv = sb("rinv", [P, RING], F32)
        identb = sb("identb", [P, P], BF16)
        maskb = sb("maskb", [P, P], BF16)

        ps_s = ps("ps_s", [P, 2, S])
        ps_t = ps("ps_t", [P, 2, 512])
        ps_m = ps("ps_m", [P, 512])
        ps_z = ps("ps_z", [P, 512])

        consts = sem("consts")
        passed = sem("passed")
        x_split = sem("x_split")
        xhi_done = sem("xhi_done2")
        proj_done = sem("proj_done")
        hi_done = sem("hi_done")
        lo_done = sem("lo_done")
        q_loaded = sem("q_loaded")
        k_loaded = sem("k_loaded")
        scores_done = sem("scores_done")
        max_done = sem("max_done")
        exp_done = sem("exp_done")
        rinv_done = sem("rinv_done")
        probs_done = sem("probs_done")
        t_done = sem("t_done")
        evac_act = sem("evac_act")
        evac_dve = sem("evac_dve")
        pv_done = sem("pv_done")
        z_done = sem("z_done")
        pw_loaded = sem("pw_loaded")
        z_moved = sem("z_moved")
        out_done = sem("out_done2")
        y_done = sem("y_done")
        gate_up_in = sem("gate_up_in")
        wgu_hi_done = sem("wgu_hi_done")
        wraw = stage[:, :, :, :].rearrange("p a b s -> p (a b s)")[:, 0:2 * NT * P].bitcast(F32).rearrange(
            "p (i j m) -> p i j m", i=2, j=NT)

        FIRST = 0

        def bank_of(k, j):
            if isinstance(k, int) and k == FIRST:
                return [ps_s[:, 0, 0:512], ps_s[:, 0, 512:S], ps_s[:, 1, 0:512], ps_s[:, 1, 512:S],
                        ps_t[:, 0, :], ps_t[:, 1, :], ps_z[:, :], ps_m[:, :]][j]
            return ps_m[:, :]

        def evacuated(n, use):
            return (evac_act if BY_ACT[use] else evac_dve), n * HALF + SEEN[use]

        def over_pairs(engine, body, tail):
            body(0, 0)
            body(1, 1)
            with engine.Fori(1, NPAIR // 2 - 1) as k:
                body(k * 2, 0)
                body(k * 2 + 1, 1)
            body(NPAIR - 2, 0)
            body(NPAIR - 1, 1)
            if tail:
                for s in range(V_LAG + 3):
                    tail(s)

        with nc.Block() as block:
            @block.gpsimd
            def _(pool):
                nc.gpsimd.memset(ident[:, :], 0.0)
                nc.gpsimd.memset(maskb[:, :], 0.0).then_inc(consts, 1)
                pool.wait_ge(consts, 1)
                nc.gpsimd.affine_select(out=ident[:, :], in_=ident[:, :], compare_op=ALU.not_equal, fill=1.0,
                                        base=0, pattern=[[-1, P]], channel_multiplier=1)
                nc.gpsimd.affine_select(out=maskb[:, :], in_=maskb[:, :], compare_op=ALU.is_ge, fill=MASKED,
                                        base=0, pattern=[[-1, P]], channel_multiplier=1).then_inc(consts, 1)
                pool.wait_ge(consts, 2)
                nc.gpsimd.tensor_copy(identb[:, :], ident[:, :]).then_inc(consts, 1)

                def body(n, par):
                    for s in range(STEPS):
                        at_least_apart(pool, rinv_done, n * STEPS + s + 1, passed)
                        row = probs[:, s % RING, 0:(s // 2 + 1) * P]
                        nc.gpsimd.tensor_scalar(row, row, rinv[:, s % RING:s % RING + 1], SCALE,
                                                ALU.mult, ALU.mult).then_inc(probs_done, 1)

                over_pairs(pool, body, None)
                pool.wait_ge(gate_up_in, 16 * 4)
                nc.gpsimd.tensor_copy(wgu[:, 0], wraw).then_inc(wgu_hi_done, 1)
                pool.wait_ge(early[0], 16 * len(early[1]))
                for i in range(2):
                    rows = y_all[:, i * TT:(i + 1) * TT, :]
                    pool.wait_ge(y_done, (i + 1) * TT)
                    nc.gpsimd.tensor_tensor(xc[i][:, :, :], xc[i][:, :, :], rows, ALU.add)
                pool.wait_ge(wgu_hi_done, 1)
                nc.gpsimd.tensor_tensor(wgu[:, 1], wraw, wgu[:, 0].bitcast(F32), ALU.subtract)

            @block.sync
            def _(sp):
                def load_weights(k, par):
                    at_least(sp, hi_done, k * 6 - 6)
                    at_least(sp, lo_done, k * 6 - 6)
                    p = k % HP
                    sp.dma_start(wbuf[par][:, :].bitcast(F32),
                                 wsp_d[bass.ds(p, 1), :, :].rearrange("o p w -> p (o w)")
                                 ).then_inc(w_loaded[par], 16)

                def load_q(k, par):
                    at_least(sp, lo_done, k * 6 + 2)
                    at_least(sp, scores_done, k * STEPS - STEPS)
                    for head in range(2):
                        for half in range(2):
                            sp.dma_start(qd[par][half * DH:(half + 1) * DH, head].bitcast(F32),
                                         stage[head * DH:(head + 1) * DH, 0].bitcast(F32)).then_inc(q_loaded, 16)

                def load_k(k, par):
                    at_least(sp, lo_done, k * 6 + 4)
                    for head in range(2):
                        for half in range(2):
                            sp.dma_start(k2[par][half * DH:(half + 1) * DH, head].bitcast(F32),
                                         stage[head * DH:(head + 1) * DH, 1, half].bitcast(F32)
                                         ).then_inc(k_loaded, 16)

                def move_z(n):
                    at_least(sp, z_done, n * 2 + 2)
                    at_least(sp, out_done, n)
                    for head in range(2):
                        for odd in range(2):
                            sp.dma_start(zs[odd * DH:(odd + 1) * DH, head],
                                         zt[head * DH:(head + 1) * DH, odd * 512:(odd + 1) * 512]
                                         ).then_inc(z_moved, 16)

                def body(n, par):
                    if exists(n + 2):
                        load_weights(n + 2, par)
                    if exists(n + 1):
                        load_q(n + 1, 1 - par)
                    if exists(n - 1):
                        move_z(n - 1)
                    if exists(n + 1):
                        load_k(n + 1, 1 - par)

                load_q(0, 0)
                load_k(0, 0)
                sp.dma_start(pw[:, :, :], proj).then_inc(pw_loaded, 16)
                for buffer, source in early[1]:
                    sp.dma_start(buffer, source).then_inc(early[0], 16)
                sp.wait_ge(w_out, 16)
                over_pairs(sp, body, None)
                sp.wait_ge(k_loaded, NPAIR * 64)
                for i, (w, ws) in enumerate(gate_up):
                    sp.dma_start(wraw[:, i, 0:NT - 1, :], w).then_inc(gate_up_in, 16)
                    sp.dma_start(wraw[:, i, NT - 1, :], ws).then_inc(gate_up_in, 16)
                move_z(NPAIR - 1)

            @block.tensor
            def _(pe):
                def project(k, par, j):
                    bank = bank_of(k, j)
                    if isinstance(k, int) and k == FIRST:
                        if j >= 6:
                            at_least(pe, hi_done, j - 1)
                    elif j == 0:
                        if isinstance(k, int) and k == 2:
                            pe.wait_ge(x_split, 1)
                        at_least(pe, w_loaded[par], (k // 2) * 16 + 16)
                        at_least(pe, lo_done, k * 6)
                    elif j <= 4:
                        at_least(pe, lo_done, k * 6 + j)
                    elif j == 5:
                        at_least(pe, hi_done, k * 6 + 5)
                    elif j == 6:
                        at_least(pe, hi_done, k * 6 + 6)
                        at_least(pe, y_done, k - 1)
                    else:
                        at_least(pe, lo_done, k * 6 + 5)
                    if j < 6:
                        which, chunk = divmod(j, 2)
                        w = [wbuf[par][:, (2 * which + i) * P:(2 * which + i + 1) * P] for i in range(2)]
                        x = [xs[:, i, bass.ds((k // HP) * S + chunk * 512, 512)] for i in range(2)]
                        nc.tensor.matmul(bank, w[0], x[0], start=True, stop=False)
                        nc.tensor.matmul(bank, w[0], x[1], start=False, stop=False)
                        nc.tensor.matmul(bank, w[1], x[0], start=False, stop=True).then_inc(proj_done, 1)
                    else:
                        for i in range(4):
                            t = (j - 6) * 4 + i
                            last = nc.tensor.transpose(bank[:, i * P:(i + 1) * P], vt[:, t * P:(t + 1) * P],
                                                       ident[:, :])
                        last.then_inc(proj_done, 1)

                def scores(n, par, s):
                    qt, head = divmod(s, 2)
                    w = (qt + 1) * P
                    if s == 0:
                        at_least(pe, q_loaded, n * 64 + 64)
                        at_least(pe, k_loaded, n * 64 + 64)
                    at_least(pe, exp_done, n * STEPS + s - 1)
                    for c0 in range(0, w, 512):
                        c1 = min(c0 + 512, w)
                        out = ps_s[:, s % 2, c0:c1]
                        keys = k2[par][:, head, c0:c1]
                        last = c1 == w
                        nc.tensor.matmul(out, qd[par][:, head, 0, qt * P:(qt + 1) * P], keys, start=True, stop=False)
                        nc.tensor.matmul(out, qd[par][:, head, 1, qt * P:(qt + 1) * P], keys, start=False,
                                         stop=not last)
                    nc.tensor.matmul(ps_s[:, s % 2, w - P:w], identb[:, :], maskb[:, :], start=False,
                                     stop=True).then_inc(scores_done, 1)

                def transpose_probs(n, s):
                    at_least(pe, probs_done, n * STEPS + s + 1)
                    qt = s // 2
                    for b in range(qt // 4 + 1):
                        use = USE_AT[s, b]
                        n0, old = (n, use - 2) if use >= 2 else (n - 1, use - 2 + NUSE)
                        at_least(pe, *evacuated(n0, old))
                        for kt in range(4 * b, min(4 * b + 4, qt + 1)):
                            last = nc.tensor.transpose(ps_t[:, use % 2, (kt % 4) * P:(kt % 4 + 1) * P],
                                                       probs[:, s % RING, kt * P:(kt + 1) * P], ident[:, :])
                        last.then_inc(t_done, 1)

                def values(n, par, m, part):
                    kts = range(m + 1) if part == 0 else range(m + 1, 2 * m + 2)
                    if part == 0 and m == 0:
                        at_least(pe, lo_done, n * 6 + 6)
                    if part == 0 and m % 2 == 0:
                        at_least(pe, z_done, n * 2 + m // 2)
                    uses = [USE_AT[s, b] for s in range(4 * m, 4 * m + 4) for b in range(s // 2 // 4 + 1)]
                    for by_act in (False, True):
                        at_least(pe, *evacuated(n, max(u for u in uses if BY_ACT[u] == by_act)))
                    for kt in kts:
                        i0 = max(kt - 2 * m, 0)
                        for head in range(2):
                            half = slice(head * DH, (head + 1) * DH)
                            last = nc.tensor.matmul(ps_z[half, (m % 2 * 2 + i0) * P:(m % 2 * 2 + 2) * P],
                                                    v[par][:, kt, half],
                                                    pt[:, head, m % 2, kt, i0:2, :].rearrange("p i q -> p (i q)"),
                                                    start=kt == 0, stop=kt == 2 * m + 1)
                    if part == 1:
                        last.then_inc(pv_done, 1)

                def project_out(n, k):
                    if exists(k):
                        at_least(pe, hi_done, k * 6 + 6)
                    else:
                        at_least(pe, lo_done, NPAIR * 6)
                        at_least(pe, y_done, n)
                    at_least(pe, z_moved, n * 64 + 64)
                    for q in range(HP):
                        for head in range(2):
                            last = nc.tensor.matmul(ps_m[head * DH:(head + 1) * DH, 0:E],
                                                    zs[:, head, q * DH:(q + 1) * DH], pw[:, q, :],
                                                    start=q == 0, stop=q == HP - 1)
                    last.then_inc(out_done, 1)

                def finish(n, par, s):
                    for part in range(2):
                        nv, odd, sv = before(n, s, V_LAG + 2 * part)
                        if sv % 4 == 2 and exists(nv):
                            values(nv, par ^ odd, sv // 4, part)
                    if s % 2 == 0 and exists(n) and exists(n + 1):
                        project(n + 1, 1 - par, s // 2)
                    if s == OUT_STEP and exists(n) and exists(n - 1):
                        project_out(n - 1, n + 1)
                    nt, odd, st = before(n, s, T_LAG)
                    if exists(nt):
                        transpose_probs(nt, st)

                def body(n, par):
                    for s in range(STEPS):
                        scores(n, par, s)
                        finish(n, par, s)

                pe.wait_ge(consts, 3)
                pe.wait_ge(w_loaded[0], 16)
                for j in range(8):
                    project(FIRST, 0, j)
                pe.wait_ge(pw_loaded, 16)
                pe.wait_ge(lo_done, 6)
                over_pairs(pe, body, lambda s: finish(NPAIR, 0, s))
                project_out(NPAIR - 1, NPAIR + 1)

            def evacuate_probs(engine, by_act, n, s):
                qt, head = divmod(s, 2)
                for b in range(qt // 4 + 1):
                    use = USE_AT[s, b]
                    if BY_ACT[use] != by_act:
                        continue
                    at_least(engine, t_done, n * NUSE + use + 1)
                    m, i = divmod(qt, 2)
                    at_least(engine, pv_done, n * MT + m - 1)
                    k0, k1 = 4 * b, min(4 * b + 4, qt + 1)
                    dst = pt[:, head, m % 2, k0:k1, i, :]
                    src = ps_t[:, use % 2, 0:(k1 - k0) * P].rearrange("p (k q) -> p k q", q=P)
                    if by_act:
                        nc.scalar.copy(dst, src).then_inc(evac_act, 1)
                    else:
                        nc.vector.tensor_copy(dst, src).then_inc(evac_dve, 1)

            def bias_of(par, which):
                return wbuf[par][:, WCOLS + which:WCOLS + which + 1].bitcast(F32)

            @block.scalar
            def _(act):
                def take_hi(k, par, j):
                    if j >= 6:
                        return
                    which, chunk = divmod(j, 2)
                    cols = slice(chunk * 512, (chunk + 1) * 512)
                    at_least(act, proj_done, k * 8 + j + 1)
                    if which < 2:
                        at_least(act, (q_loaded, k_loaded)[which], k * 64)
                        dst = stage[:, which, 0, cols]
                    else:
                        dst = vt[:, cols]
                    nc.scalar.activation(dst, bank_of(k, j), ACT.Identity, bias=bias_of(par, which)).then_inc(hi_done, 1)

                def exponentials(n, s):
                    n4, _, s4 = before(n, s, RING)
                    at_least(act, max_done, n * STEPS + s + 1)
                    if exists(n4):
                        at_least(act, t_done, n4 * NUSE + USE_AT[s4, s4 // 2 // 4] + 1)
                    w = (s // 2 + 1) * P
                    nc.scalar.activation(probs[:, s % RING, 0:w], ps_s[:, s % 2, 0:w], ACT.Exp,
                                         bias=negmax[:, s % RING:s % RING + 1],
                                         accum_out=rowsum[:, s % RING:s % RING + 1]).then_inc(exp_done, 1)

                def evacuate_z(n, half):
                    at_least(act, pv_done, n * MT + 2 * half + 2)
                    if half == 0:
                        at_least(act, z_moved, n * 64)
                    dst = zt[:, :].rearrange("p (o q i) -> p o q i", o=2, q=HP)[:, :, :, half * 32:(half + 1) * 32]
                    src = ps_z[:, :].rearrange("p (i q o) -> p o q i", q=HP, o=2)
                    nc.scalar.copy(dst, src).then_inc(z_done, 1)

                def take_out(n):
                    at_least(act, out_done, n + 1)
                    nc.scalar.copy(y_all[:, bass.ds(n, 1), :].rearrange("p o e -> p (o e)"),
                                   ps_m[:, 0:E]).then_inc(y_done, 1)

                def finish(n, par, s):
                    if s == Z_STEPS[0] and exists(n):
                        evacuate_z(n, 0)
                    if s == Z_STEPS[1] and exists(n - 1):
                        evacuate_z(n - 1, 1)
                    if s == OUT_STEP and exists(n) and exists(n - 1):
                        take_out(n - 1)
                    nt, _, st = before(n, s, T_LAG)
                    if exists(nt):
                        evacuate_probs(act, True, nt, st)

                def body(n, par):
                    for s in range(STEPS):
                        if s % 2 == 0 and exists(n + 1):
                            take_hi(n + 1, 1 - par, s // 2)
                        exponentials(n, s)
                        finish(n, par, s)

                for j in range(8):
                    take_hi(FIRST, 0, j)
                act.wait_ge(w_out, 16)
                act.wait_ge(x_in[1], 16)
                nc.scalar.activation(xs[:, 0, S:T_ALL], xraw[:, S:T_ALL], ACT.Copy).then_inc(xhi_done, 1)
                over_pairs(act, body, lambda s: finish(NPAIR, 0, s))
                take_out(NPAIR - 1)

            @block.vector
            def _(dve):
                def take_lo(k, par, j):
                    if j in (4, 5):
                        return
                    if j < 4:
                        which, chunk = divmod(j, 2)
                        cols = slice(chunk * 512, (chunk + 1) * 512)
                        at_least(dve, hi_done, k * 6 + j + 1)
                        nc.vector.scalar_tensor_tensor(out=stage[:, which, 1, cols], in0=bank_of(k, j),
                                                       scalar=bias_of(par, which),
                                                       in1=stage[:, which, 0, cols].bitcast(F32),
                                                       op0=ALU.add, op1=ALU.subtract).then_inc(lo_done, 1)
                    else:
                        at_least(dve, proj_done, k * 8 + j + 1)
                        at_least(dve, pv_done, k * MT - MT)
                        tiles = v[par][:, (j - 6) * 4:(j - 6) * 4 + 4, :].rearrange("p t d -> p (t d)")
                        nc.vector.tensor_copy(tiles, bank_of(k, j)).then_inc(lo_done, 1)

                def maxima(n, s):
                    at_least(dve, scores_done, n * STEPS + s + 1)
                    nc.vector.tensor_reduce(negmax[:, s % RING:s % RING + 1], ps_s[:, s % 2, 0:(s // 2 + 1) * P],
                                            AX.X, ALU.max, negate=True).then_inc(max_done, 1)

                def reciprocals(n, s):
                    at_least(dve, exp_done, n * STEPS + s + 1)
                    nc.vector.reciprocal(rinv[:, s % RING:s % RING + 1], rowsum[:, s % RING:s % RING + 1]).then_inc(rinv_done, 1)

                def finish(n, par, s):
                    n1, _, s1 = before(n, s, 1)
                    if exists(n1) and (s == 0 or exists(n)):
                        reciprocals(n1, s1)
                    nt, _, st = before(n, s, T_LAG)
                    if exists(nt):
                        evacuate_probs(dve, False, nt, st)

                def body(n, par):
                    for s in range(STEPS):
                        if s % 2 == 1 and exists(n + 1) and s // 2 < 4:
                            take_lo(n + 1, 1 - par, s // 2)
                        maxima(n, s)
                        if s % 2 == 1 and exists(n + 1) and s // 2 >= 4:
                            take_lo(n + 1, 1 - par, s // 2)
                        finish(n, par, s)

                for j in range(8):
                    take_lo(FIRST, 0, j)
                dve.wait_ge(w_out, 16)
                dve.wait_ge(xhi_done, 1)
                nc.vector.tensor_tensor(xs[:, 1, S:T_ALL], xraw[:, S:T_ALL], xs[:, 0, S:T_ALL].bitcast(F32),
                                        ALU.subtract).then_inc(x_split, 1)
                over_pairs(dve, body, lambda s: finish(NPAIR, 0, s))


def mixture(nc, y_all, xc, wgu, wd, gw, ident, x_tok, out):
    with ExitStack() as c:
        def sb(name, shape, dt=F32):
            return c.enter_context(nc.sbuf_tensor(name, shape, dt))

        def ps(name):
            return c.enter_context(nc.psum_tensor(name, [P, 512], F32))

        def sem(name):
            return c.enter_context(nc.semaphore(name))

        x1 = [sb(f"x1{i}", [P, TT, E]) for i in range(2)]
        xn = [sb(f"xn{i}", [P, 2, CHUNK], F32R) for i in range(2)]
        res = sb("res", [P, TT, E])
        ob = [sb(f"ob{i}", [P, TT, E]) for i in range(2)]
        stats = sb("stats", [P, 2, TT, 6])
        mv = sb("mv", [P, 2, TT, 2])
        veps = sb("veps", [P, 2, TT, 1])
        rstd = sb("rstd", [P, 2, TT, 1])
        nmax = sb("nmax", [P, TT, 1])
        logit = sb("logit", [P, TT, NE])
        lg = sb("lg", [P, TT, NE])
        ex = sb("ex", [P, TT, NE])
        esum = sb("esum", [P, TT, 1])
        einv = sb("einv", [P, TT, 1])
        sc = sb("sc", [P, TT, NE])
        top = sb("top", [P, TT, 8])
        topi = sb("topi", [P, TT, 8], U32)
        topf = sb("topf", [P, TT, 8])
        hit = sb("hit", [P, TT, 2, NE])
        won = sb("won", [P, TT, 2, NE])
        comb = sb("comb", [P, TT, NE])
        cc = sb("cc", [P, TT, P], F32R)
        cT = [sb(f"cT{i}", [P, CHUNK], F32R) for i in range(2)]
        sel = sb("sel", [P, NT - 1, P], F32R)
        iota = sb("iota", [P, TT, 2, NE])
        epst = sb("epst", [P, TT, 1])
        mhalf = sb("mhalf", [P, TT, 1])
        gs = sb("gs", [P, 2, NE], F32R)
        sg = sb("sg", [P, 2, CHUNK])
        su = sb("su", [P, 2, CHUNK])
        hid = sb("hid", [P, NT, CHUNK])

        ps_x, ps_d = ps("ps_x"), ps("ps_d")
        ps_b = [ps("ps_b0"), ps("ps_b1")]
        ps_g = [ps("ps_g0"), ps("ps_g1")]
        ps_u = [ps("ps_u0"), ps("ps_u1")]

        consts = sem("consts3")
        gs_done = sem("gs_done")
        passed_dve = sem("passed_dve")
        passed_pool = sem("passed_pool")
        chunk_in = [sem(f"chunk_in{i}") for i in range(2)]
        sum_done = sem("sum_done")
        first_stats = sem("first_stats")
        first_var = sem("first_var")
        last_sum = sem("last_sum")
        last_stats = sem("last_stats")
        last_var = sem("last_var")
        rstd_steps = [sem(f"rstd_steps{i}") for i in range(2)]
        x1_done = sem("x1_done")
        xt_done = sem("xt_done")
        xhi_done = sem("xhi_done")
        xlo_done = sem("xlo_done")
        logit_done = sem("logit_done")
        lg_done = sem("lg_done")
        ex_done = sem("ex_done")
        gate_steps = sem("gate_steps")
        comb_done = sem("comb_done")
        cc_done = sem("cc_done")
        wt_done = sem("wt_done")
        ct_done = sem("ct_done")
        g_done = sem("g_done")
        u_done = sem("u_done")
        b_done = sem("b_done")
        silu_done = sem("silu_done")
        su_done = sem("su_done")
        hid_done = sem("hid_done")
        down_done = sem("down_done")
        out_done = sem("out_done")
        stored = sem("stored")

        def over_chunks(engine, front, experts):
            front(0, 0)
            experts(0, 0)
            experts(1, 1)
            with engine.Fori(1, NCH // 2 - 1) as k:
                experts(k * 2, 0)
                experts(k * 2 + 1, 1)
            experts(NCH - 2, 0)
            experts(NCH - 1, 1)

        with nc.Block() as block:
            @block.sync
            def _(sp):
                def load(c, par):
                    at_least(sp, x1_done, c - 1)
                    sp.dma_start(xc[par][:, :, :], x_tok.rearrange("(c t p) e -> c p t e", t=TT, p=P)
                                 [bass.ds(c, 1)].rearrange("o p t e -> p (o t) e")).then_inc(chunk_in[par], 16)

                def store(c, par):
                    at_least(sp, out_done, c + 1)
                    sp.dma_start(out.rearrange("(c t p) e -> c p t e", t=TT, p=P)
                                 [bass.ds(c, 1)].rearrange("o p t e -> p (o t) e"), ob[par][:, :, :]
                                 ).then_inc(stored, 16)

                load(2, 0)
                load(3, 1)
                store(0, 0)
                store(1, 1)
                with sp.Fori(1, NCH // 2 - 1) as k:
                    load(k * 2 + 2, 0)
                    load(k * 2 + 3, 1)
                    store(k * 2, 0)
                    store(k * 2 + 1, 1)
                store(NCH - 2, 0)
                store(NCH - 1, 1)
                sp.wait_ge(stored, 16 * NCH)

            @block.gpsimd
            def _(pool):
                def deviation(c, which, var):
                    at_least(pool, var, c + 1)
                    nc.gpsimd.tensor_tensor(veps[:, which], mv[:, which, :, 1:2], epst[:, :, :],
                                            ALU.add).then_inc(rstd_steps[which], 1)
                    at_least(pool, rstd_steps[which], c * 2 + 1)
                    nc.gpsimd.tensor_tensor(rstd[:, which], veps[:, which], mhalf[:, :, :],
                                            ALU.pow).then_inc(rstd_steps[which], 1)

                def normalise(c, which, src, dst, done):
                    at_least_apart(pool, rstd_steps[which], c * 2 + 2, passed_pool)
                    for t in range(TT):
                        last = nc.gpsimd.tensor_scalar(dst[:, t, :], src[:, t, :], mv[:, which, t, 0:1],
                                                       rstd[:, which, t, 0:1], ALU.subtract, ALU.mult)
                    last.then_inc(done, 1)

                def first_norm(c, par):
                    deviation(c, 0, first_var)
                    at_least_apart(pool, last_sum, c - 1, passed_pool)
                    normalise(c, 0, xc[par], x1[par], x1_done)

                def last_norm(c, par):
                    deviation(c, 1, last_var)
                    at_least_apart(pool, stored, c * 16, passed_pool)
                    normalise(c, 1, res, ob[par], out_done)

                def first_sum(c, par):
                    at_least(pool, chunk_in[par], (c // 2) * 16)
                    nc.gpsimd.tensor_tensor(xc[par][:, :, :], xc[par][:, :, :], y_all[:, bass.ds(c * TT, TT), :],
                                            ALU.add).then_inc(sum_done, 1)

                def experts(c, par):
                    if chunk_exists(c + 1):
                        first_norm(c + 1, 1 - par)
                    if chunk_exists(c - 1):
                        last_norm(c - 1, 1 - par)
                    if chunk_exists(c + 2):
                        first_sum(c + 2, par)

                def front(c, par):
                    deviation(c, 0, first_var)
                    for i in range(2):
                        pool.wait_ge(consts, i + 2)
                        nc.gpsimd.affine_select(out=raw_sel, in_=raw_sel, compare_op=ALU.not_equal, fill=1.0,
                                                base=-i * NE, pattern=[[-2, NT - 1], [-1, 2], [0, NI]],
                                                channel_multiplier=1).then_inc(consts, 1)
                    pool.wait_ge(consts, 4)
                    nc.gpsimd.tensor_copy(sel[:, :, :].rearrange("p j m -> p (j m)"),
                                          hid[:, 0:2, :].rearrange("p j m -> p (j m)")).then_inc(consts, 1)

                raw_sel = hid[:, 0:2, :].rearrange("p a m -> p (a m)").rearrange(
                    "p (j e i) -> p j e i", j=NT - 1, e=2)
                nc.gpsimd.memset(epst[:, :, :], EPS)
                nc.gpsimd.memset(mhalf[:, :, :], -0.5)
                nc.gpsimd.iota(iota[:, :, :, :], pattern=[[0, 2 * TT], [1, NE]], base=0, channel_multiplier=0,
                               allow_small_or_imprecise_dtypes=True)
                nc.gpsimd.memset(cc[:, :, :].bitcast(F32), 0.0).then_inc(consts, 1)
                nc.gpsimd.memset(raw_sel, 0.0).then_inc(consts, 1)
                pool.wait_ge(consts, 1)
                over_chunks(pool, front, experts)
                deviation(NCH - 1, 1, last_var)

            @block.tensor
            def _(pe):
                def first_transpose(c, par):
                    at_least(pe, x1_done, c + 1)
                    at_least(pe, ct_done, c)
                    for t in range(TT):
                        last = nc.tensor.transpose(ps_x[:, t * P:(t + 1) * P], x1[par][:, t, :], ident[:, :])
                    last.then_inc(xt_done, 1)

                def logits(c, par):
                    at_least(pe, xhi_done, c + 1)
                    at_least(pe, xlo_done, c + 1)
                    for t in range(TT):
                        for i in range(2):
                            last = nc.tensor.matmul(ps_x[:, t * 2 * NE:(t + 1) * 2 * NE],
                                                    xn[par][:, i, t * P:(t + 1) * P],
                                                    gs[:, :, :].rearrange("p h e -> p (h e)"),
                                                    start=i == 0, stop=i == 1)
                    last.then_inc(logit_done, 1)

                def weights_transpose(c):
                    at_least(pe, cc_done, c + 1)
                    for t in range(TT):
                        last = nc.tensor.transpose(ps_x[:, t * P:(t + 1) * P], cc[:, t, :].bitcast(F32), ident[:, :])
                    last.then_inc(wt_done, 1)

                def gate_up(c, par, j):
                    r = (j + par) % 2
                    for which, banks, done in ((0, ps_g, g_done), (1, ps_u, u_done)):
                        if which == 0:
                            at_least(pe, silu_done, c * NT + max(j - 1, 0))
                        else:
                            at_least(pe, hid_done, c * NT + max(j - 1, 0))
                        for i, (a, b) in enumerate(((0, 0), (0, 1), (1, 0))):
                            last = nc.tensor.matmul(banks[r][:, :], wgu[:, a, which, j, :], xn[par][:, b, :],
                                                    start=i == 0, stop=i == 2)
                        last.then_inc(done, 1)

                def weights(c, par, j):
                    r = (j + par) % 2
                    if j < NT - 1:
                        if j == 0:
                            at_least(pe, ct_done, c + 1)
                        nc.tensor.matmul(ps_b[r][:, :], sel[:, j, :], cT[par][:, :], start=True,
                                         stop=True).then_inc(b_done, 1)

                def down(c, par):
                    at_least(pe, hid_done, c * NT + NT - 1)
                    at_least(pe, last_sum, c)
                    for t in range(TT):
                        for j in range(NT):
                            if t == 0 and j == NT - 1:
                                at_least(pe, hid_done, c * NT + NT)
                            last = nc.tensor.matmul(ps_d[:, t * P:(t + 1) * P], hid[:, j, t * P:(t + 1) * P],
                                                    wd[:, j, :], start=j == 0, stop=j == NT - 1)
                    last.then_inc(down_done, 1)

                def experts(c, par):
                    for j in range(NT):
                        if not (isinstance(c, int) and c == 0 and j < 2):
                            gate_up(c, par, j)
                        weights(c, par, j)
                        if chunk_exists(c + 1) and j == 4:
                            first_transpose(c + 1, 1 - par)
                        if chunk_exists(c + 1) and j == 7:
                            logits(c + 1, 1 - par)
                    down(c, par)
                    if chunk_exists(c + 1):
                        weights_transpose(c + 1)

                def front(c, par):
                    first_transpose(c, par)
                    logits(c, par)
                    for j in range(2):
                        gate_up(c, par, j)
                    weights_transpose(c)
                    pe.wait_ge(consts, 5)

                pe.wait_ge(gs_done, 2)
                over_chunks(pe, front, experts)

            @block.scalar
            def _(act):
                def take_xhi(c, par):
                    at_least(act, xt_done, c + 1)
                    nc.scalar.copy(xn[par][:, 0, :], ps_x[:, :]).then_inc(xhi_done, 1)

                def gate_exp(c):
                    at_least(act, lg_done, c + 1)
                    nc.scalar.activation(ex[:, :, :], lg[:, :, :], ACT.Exp).then_inc(ex_done, 1)

                def take_weights(c, par):
                    at_least(act, wt_done, c + 1)
                    nc.scalar.copy(cT[par][:, :], ps_x[:, :]).then_inc(ct_done, 1)

                def tile(c, par, j):
                    at_least(act, g_done, c * NT + j + 1)
                    at_least(act, hid_done, c * NT + max(j - 1, 0))
                    r = (j + par) % 2
                    nc.scalar.activation(sg[:, r, :], ps_g[r][:, :], ACT.Silu).then_inc(silu_done, 1)

                def experts(c, par):
                    for j in range(NT):
                        tile(c, par, j)
                        if chunk_exists(c + 1) and j == 4:
                            take_xhi(c + 1, 1 - par)
                    if chunk_exists(c + 1):
                        gate_exp(c + 1)
                        take_weights(c + 1, 1 - par)

                def front(c, par):
                    take_xhi(c, par)
                    gate_exp(c)
                    take_weights(c, par)

                nc.scalar.copy(gs[:, 0, :], gw[:, :]).then_inc(gs_done, 1)
                over_chunks(act, front, experts)

            @block.vector
            def _(dve):
                GATE = 10

                def statistics(which, src, done):
                    for t in range(TT):
                        last = nc.vector.bn_stats(stats[:, which, t, :], src[:, t, :])
                    last.then_inc(done, 1)

                def moments(c, which, stats_done, var):
                    at_least_apart(dve, stats_done, c + 1, passed_dve)
                    for t in range(TT):
                        last = nc.vector.bn_aggr(mv[:, which, t, :], stats[:, which, t, :])
                    last.then_inc(var, 1)

                def normalise(c, which, src, dst, done):
                    dve.wait_ge(rstd_steps[which], c * 2 + 2)
                    for t in range(TT):
                        last = nc.vector.tensor_scalar(dst[:, t, :], src[:, t, :], mv[:, which, t, 0:1],
                                                       rstd[:, which, t, 0:1], ALU.subtract, ALU.mult)
                    last.then_inc(done, 1)

                def first_moments(c, par):
                    at_least_apart(dve, sum_done, c - 1, passed_dve)
                    statistics(0, xc[par], first_stats)
                    moments(c, 0, first_stats, first_var)

                def sum_down(c, par):
                    at_least(dve, down_done, c + 1)
                    at_least(dve, out_done, c)
                    nc.vector.tensor_tensor(res[:, :, :].rearrange("p t e -> p (t e)"), ps_d[:, :],
                                            x1[par][:, :, :].rearrange("p t e -> p (t e)"),
                                            ALU.add).then_inc(last_sum, 1)

                def last_statistics(c):
                    at_least_apart(dve, last_sum, c + 1, passed_dve)
                    statistics(1, res, last_stats)

                def take_xlo(c, par):
                    at_least(dve, xhi_done, c + 1)
                    nc.vector.tensor_tensor(xn[par][:, 1, :], ps_x[:, :], xn[par][:, 0, :].bitcast(F32),
                                            ALU.subtract).then_inc(xlo_done, 1)

                def gate_logits(c):
                    at_least(dve, logit_done, c + 1)
                    parts = ps_x[:, 0:TT * 2 * NE].rearrange("p (t h e) -> p t e h", t=TT, h=2)
                    nc.vector.tensor_reduce(logit[:, :, :], parts, AX.X, ALU.add).then_inc(gate_steps, 1)
                    at_least(dve, gate_steps, c * GATE + 1)
                    nc.vector.tensor_reduce(nmax[:, :, 0], logit[:, :, :], AX.X, ALU.max).then_inc(gate_steps, 1)
                    at_least(dve, gate_steps, c * GATE + 2)
                    nc.vector.tensor_tensor(lg[:, :, :], logit[:, :, :], nmax[:, :, :].to_broadcast([P, TT, NE]),
                                            ALU.subtract).then_inc(lg_done, 1)

                def gates(c):
                    at_least(dve, ex_done, c + 1)
                    nc.vector.tensor_reduce(esum[:, :, 0], ex[:, :, :], AX.X, ALU.add).then_inc(gate_steps, 1)
                    at_least(dve, gate_steps, c * GATE + 3)
                    nc.vector.reciprocal(einv[:, :, :], esum[:, :, :]).then_inc(gate_steps, 1)
                    at_least(dve, gate_steps, c * GATE + 4)
                    nc.vector.tensor_tensor(sc[:, :, :], ex[:, :, :], einv[:, :, :].to_broadcast([P, TT, NE]),
                                            ALU.mult).then_inc(gate_steps, 1)
                    at_least_apart(dve, gate_steps, c * GATE + 5, passed_dve)
                    for t in range(TT):
                        last = nc.vector.max(top[:, t, :], sc[:, t, :])
                    last.then_inc(gate_steps, 1)
                    at_least_apart(dve, gate_steps, c * GATE + 6, passed_dve)
                    for t in range(TT):
                        last = nc.vector.max_index(topi[:, t, :], top[:, t, :], sc[:, t, :])
                    last.then_inc(gate_steps, 1)
                    at_least(dve, gate_steps, c * GATE + 7)
                    nc.vector.tensor_copy(topf[:, :, :], topi[:, :, :]).then_inc(gate_steps, 1)
                    at_least(dve, gate_steps, c * GATE + 8)
                    for i in range(2):
                        chosen = topf[:, :, i:i + 1].to_broadcast([P, TT, NE])
                        last = nc.vector.tensor_tensor(hit[:, :, i, :], iota[:, :, i, :], chosen, ALU.is_equal)
                    last.then_inc(gate_steps, 1)
                    at_least(dve, gate_steps, c * GATE + 9)
                    for i in range(2):
                        last = nc.vector.tensor_tensor(won[:, :, i, :], hit[:, :, i, :],
                                                       top[:, :, i:i + 1].to_broadcast([P, TT, NE]), ALU.mult)
                    last.then_inc(gate_steps, 1)
                    at_least(dve, gate_steps, c * GATE + 10)
                    nc.vector.tensor_tensor(comb[:, :, :], won[:, :, 0, :], won[:, :, 1, :], ALU.add)
                    nc.vector.tensor_tensor(cc[:, :, 0:NE], won[:, :, 0, :], won[:, :, 1, :],
                                            ALU.add).then_inc(comb_done, 1)
                    at_least(dve, comb_done, c + 1)
                    nc.vector.tensor_tensor(cc[:, :, NE:2 * NE], comb[:, :, :], cc[:, :, 0:NE].bitcast(F32),
                                            ALU.subtract).then_inc(cc_done, 1)

                def tile(c, par, j):
                    r = (j + par) % 2
                    at_least(dve, silu_done, c * NT + j + 1)
                    at_least(dve, u_done, c * NT + j + 1)
                    if j == 0:
                        at_least(dve, down_done, c)
                    if j == NT - 1:
                        nc.vector.tensor_tensor(hid[:, j, :], sg[:, r, :], ps_u[r][:, :],
                                                ALU.mult).then_inc(hid_done, 1)
                        return
                    nc.vector.tensor_tensor(su[:, r, :], sg[:, r, :], ps_u[r][:, :], ALU.mult).then_inc(su_done, 1)
                    at_least(dve, su_done, c * (NT - 1) + j + 1)
                    at_least(dve, b_done, c * (NT - 1) + j + 1)
                    nc.vector.tensor_tensor(hid[:, j, :], su[:, r, :], ps_b[r][:, :], ALU.mult).then_inc(hid_done, 1)

                def experts(c, par):
                    for j in range(NT):
                        tile(c, par, j)
                        if chunk_exists(c - 1) and j == 0:
                            sum_down(c - 1, 1 - par)
                        if chunk_exists(c - 1) and j == 1:
                            last_statistics(c - 1)
                        if chunk_exists(c - 1) and j == 2:
                            moments(c - 1, 1, last_stats, last_var)
                        if chunk_exists(c + 1) and j == 4:
                            take_xlo(c + 1, 1 - par)
                    if chunk_exists(c + 1):
                        gate_logits(c + 1)
                        gates(c + 1)
                    if chunk_exists(c + 2):
                        first_moments(c + 2, par)

                def front(c, par):
                    first_moments(c, par)
                    normalise(c, 0, xc[par], x1[par], x1_done)
                    take_xlo(c, par)
                    gate_logits(c)
                    gates(c)
                    first_moments(c + 1, 1 - par)

                dve.wait_ge(gs_done, 1)
                nc.vector.tensor_tensor(gs[:, 1, :], gw[:, :], gs[:, 0, :].bitcast(F32),
                                        ALU.subtract).then_inc(gs_done, 1)
                over_chunks(dve, front, experts)
                c, par = NCH - 1, (NCH - 1) % 2
                sum_down(c, par)
                last_statistics(c)
                moments(c, 1, last_stats, last_var)
                normalise(c, 1, res, ob[par], out_done)


def layer(nc, xT, x_tok, wq, wk, wv, bq, bk, bv, proj, gate_w, w_gate, w_up, w_down, ws_gate, ws_up, ws_down, out):
    wsp_d = nc.dram_tensor("wsp_d", (HP, P, WROW), F32).ap()
    with ExitStack() as ctx:
        def sb(name, shape):
            return ctx.enter_context(nc.sbuf_tensor(name, shape, F32))

        y_all = sb("y_all", [P, NPAIR, E])
        xc = [sb(f"xc{i}", [P, TT, E]) for i in range(2)]
        xs = ctx.enter_context(nc.sbuf_tensor("xs", [P, 2, T_ALL], F32R))
        wgu = xs[:, :, :].rearrange("p h t -> p (h t)")[:, 0:4 * NT * P].rearrange(
            "p (h i j m) -> p h i j m", h=2, i=2, j=NT)
        wd = sb("wd", [P, NT, E])
        gw = sb("gw", [P, NE])
        ident = sb("ident", [P, P])
        early = ctx.enter_context(nc.semaphore("early"))
        chunks = x_tok.rearrange("(c t p) e -> c p t e", t=TT, p=P)
        loads = [(gw[:, :], gate_w), (wd[:, 0:NT - 1, :], w_down), (wd[:, NT - 1, :], ws_down)]
        loads += [(xc[i][:, :, :], chunks[i]) for i in range(2)]

        with ExitStack() as inner:
            wbuf = [inner.enter_context(nc.sbuf_tensor(f"wbuf{i}", [P, WROW], F32R)) for i in range(2)]
            w_loaded = [inner.enter_context(nc.semaphore(f"w_loaded{i}")) for i in range(2)]
            x_in = [inner.enter_context(nc.semaphore(f"x_in{i}")) for i in range(2)]
            xraw = y_all[:, :, :].rearrange("p n e -> p (n e)")
            pt = inner.enter_context(nc.sbuf_tensor("pt", [P, 2, 2, QT, 2, P], F32))
            wsp = pt[:, :, :, :, :, :].rearrange("p a b k i q -> p (a b k i q)")[:, 0:HP * WROW].bitcast(
                F32R).rearrange("p (n w) -> p n w", n=HP)
            w_out = inner.enter_context(nc.semaphore("w_out"))
            split_inputs(nc, xs, xraw, wbuf, w_loaded, x_in, wsp, wsp_d, w_out, xT, wq, wk, wv, bq, bk, bv)
            attention(nc, xs, xraw, wbuf, w_loaded, x_in, pt, wsp_d, w_out, proj, y_all, ident, wgu,
                      ((w_gate, ws_gate), (w_up, ws_up)), xc, (early, loads))
        mixture(nc, y_all, xc, wgu, wd, gw, ident, x_tok, out)


def kernel(**inputs):
    import numpy as _np
    import concourse.bacc as _bacc
    from concourse import mybir as _mybir
    from concourse.bass_utils import run_bass_kernel_spmd as _run

    a = {k: _np.asarray(v) for k, v in inputs.items()}
    x = a["L0_attn_x"].reshape(T_ALL, E)

    def by_pair(w):
        return w.reshape(HP, P, E).transpose(2, 0, 1)

    def by_tile(w):
        return w.transpose(1, 0, 2).reshape(E, NT - 1, P)

    arrays = {
        "xT": x.T,
        "x_tok": x,
        "wq": by_pair(a["L0_attn_Wq"]),
        "wk": by_pair(a["L0_attn_Wk"]),
        "wv": by_pair(a["L0_attn_Wv"]),
        "bq": a["L0_attn_bq"].reshape(HP, P).T,
        "bk": a["L0_attn_bk"].reshape(HP, P).T,
        "bv": a["L0_attn_bv"].reshape(HP, P).T,
        "proj": a["L0_attn_proj"].reshape(HP, P, E).transpose(1, 0, 2),
        "gate_w": a["L0_ffn_gate_w"].T,
        "w_gate": by_tile(a["L0_ffn_w_gate"]),
        "w_up": by_tile(a["L0_ffn_w_up"]),
        "w_down": a["L0_ffn_w_down"].reshape(NT - 1, P, E).transpose(1, 0, 2),
        "ws_gate": a["L0_ffn_ws_gate"],
        "ws_up": a["L0_ffn_ws_up"],
        "ws_down": a["L0_ffn_ws_down"],
    }
    arrays = {k: _np.ascontiguousarray(v) for k, v in arrays.items()}
    nc = _bacc.Bacc("TRN2", target_bir_lowering=False, num_devices=1)
    args = [nc.dram_tensor(k, v.shape, _mybir.dt.from_np(v.dtype), kind="ExternalInput").ap()
            for k, v in arrays.items()]
    out = nc.dram_tensor("out", (T_ALL, E), _mybir.dt.float32, kind="ExternalOutput").ap()
    layer(nc, *args, out)
    r = _run(nc, [arrays], core_ids=[0])
    return r.results[0]["out"].reshape(B, S, E)
```
